# Optimizing a Trainium2 kernel written in Bass

```python
import numpy as np
import jax
import jax.numpy as jnp

def _softmax(x, axis=-1):
    return jax.nn.softmax(x, axis=axis)

def _gelu(x):
    return jax.nn.gelu(x, approximate=True)

def _silu(x):
    return jax.nn.silu(x)

def _sigmoid(x):
    return jax.nn.sigmoid(x)

def _layernorm(x, axis=-1, eps=1e-05):
    m = jnp.mean(x, axis=axis, keepdims=True)
    v = jnp.var(x, axis=axis, keepdims=True)
    return (x - m) / jnp.sqrt(v + eps)

def _scatter_add(tgt, idx, src, axis=0):
    return tgt.at[idx].add(src)

def _segment_sum(src, seg, n):
    return jax.ops.segment_sum(src, seg, n)
kernel_name = 'mk_vit_tower_postln_d1_tok_img256_r4_32b039'

def setup_inputs(seed: int=0):
    np.random.seed(seed)
    _w = jnp.asarray

    def _rec_inputs():
        import jax
        import jax.numpy as jnp
        _rk = jax.random.key(seed)
        x = -7.10856e-05 + 0.999911 * jax.random.normal(jax.random.fold_in(_rk, 1), (2, 64, 128, 64), jnp.float32)
        return x
    x = _rec_inputs()

    def _L0_tok_setup():
        import jax, jax.numpy as jnp
        import numpy as np
        PATCH_LEN = 16
        STRIDE = 8
        PAD = 8
        key = jax.random.key(seed)
        k1, k2 = jax.random.split(key)
        x = jax.random.normal(k1, (32, 64, 128, 64), dtype=jnp.float32)
        in_feat = 64 * (PATCH_LEN // 2 + 1) * 2
        W = jax.random.normal(k2, (64, in_feat), dtype=jnp.float32) * 0.02
        return {'x': x, 'W': W}
    _L0_tok_all = _L0_tok_setup()
    _L0_tok_in = {k: v for k, v in _L0_tok_all.items() if k in ('W',)}
    del _L0_tok_all

    def _L0_attn_setup():
        import jax, jax.numpy as jnp
        import numpy as np
        GAMMA = 0.96875
        ROPE_THETA = 10000.0

        def _rope(x):
            B, S, d = x.shape
            inv_freq = 1.0 / ROPE_THETA ** (jnp.arange(0, d, 2, dtype=jnp.float32) / d)
            angles = jnp.arange(S, dtype=jnp.float32)[:, None] * inv_freq[None, :]
            cos = jnp.cos(angles).astype(x.dtype)
            sin = jnp.sin(angles).astype(x.dtype)
            xs = x.reshape(B, S, d // 2, 2)
            x0, x1 = (xs[..., 0], xs[..., 1])
            out = jnp.stack([x0 * cos - x1 * sin, x1 * cos + x0 * sin], axis=-1)
            return out.reshape(B, S, d)

        def _decay_mask(S, dtype):
            n = jnp.arange(S)[:, None]
            m = jnp.arange(S)[None, :]
            diff = n - m
            D = jnp.exp(jnp.maximum(diff, 0).astype(jnp.float32) * np.log(GAMMA))
            return jnp.where(diff >= 0, D, 0.0).astype(dtype)
        key = jax.random.key(seed)
        k1, k2, k3, k4 = jax.random.split(key, 4)
        H = 64
        X = jax.random.normal(k1, (4, 2048, H), dtype=jnp.float32)
        W_Q = jax.random.normal(k2, (H, H), dtype=jnp.float32) / H
        W_K = jax.random.normal(k3, (H, H), dtype=jnp.float32) / H
        W_V = jax.random.normal(k4, (H, H), dtype=jnp.float32) / H
        return {'X': X, 'W_Q': W_Q, 'W_K': W_K, 'W_V': W_V}
    _L0_attn_all = _L0_attn_setup()
    _L0_attn_in = {k: v for k, v in _L0_attn_all.items() if k in ('W_Q', 'W_K', 'W_V')}
    del _L0_attn_all

    def _L0_ffn_setup():
        import jax, jax.numpy as jnp
        import numpy as np
        B, T, IN_DIM = (64, 64, 64)
        HID, OUT_DIM = (128, 64)
        N_LAYERS, N_EXPERTS, N_SHARED = (2, 16, 1)
        key = jax.random.key(seed)
        ks = jax.random.split(key, 10)
        s = 0.02
        x = jax.random.normal(ks[0], (B, T, IN_DIM), dtype=jnp.float32)
        route_id = jax.random.randint(ks[1], (B,), 0, N_EXPERTS)
        Wi = jax.random.normal(ks[2], (HID, IN_DIM), dtype=jnp.float32) * s
        bi = jnp.zeros((HID,), dtype=jnp.float32)
        Wr = jax.random.normal(ks[3], (N_LAYERS, N_EXPERTS, HID, HID), dtype=jnp.float32) * s
        br = jax.random.normal(ks[4], (N_LAYERS, N_EXPERTS, HID), dtype=jnp.float32) * s
        Ws = jax.random.normal(ks[5], (N_LAYERS, N_SHARED, HID, HID), dtype=jnp.float32) * s
        bs = jax.random.normal(ks[6], (N_LAYERS, N_SHARED, HID), dtype=jnp.float32) * s
        Wo = jax.random.normal(ks[7], (OUT_DIM, HID), dtype=jnp.float32) * s
        bo = jnp.zeros((OUT_DIM,), dtype=jnp.float32)
        return {'x': x, 'route_id': route_id, 'Wi': Wi, 'bi': bi, 'Wr': Wr, 'br': br, 'Ws': Ws, 'bs': bs, 'Wo': Wo, 'bo': bo}
    _L0_ffn_all = _L0_ffn_setup()
    _L0_ffn_in = {k: v for k, v in _L0_ffn_all.items() if k in ('route_id', 'Wi', 'bi', 'Wr', 'br', 'Ws', 'bs', 'Wo', 'bo')}
    del _L0_ffn_all
    return {'x': x, 'L0_tok_W': _L0_tok_in['W'], 'L0_attn_W_Q': _L0_attn_in['W_Q'], 'L0_attn_W_K': _L0_attn_in['W_K'], 'L0_attn_W_V': _L0_attn_in['W_V'], 'L0_ffn_route_id': _L0_ffn_in['route_id'], 'L0_ffn_Wi': _L0_ffn_in['Wi'], 'L0_ffn_bi': _L0_ffn_in['bi'], 'L0_ffn_Wr': _L0_ffn_in['Wr'], 'L0_ffn_br': _L0_ffn_in['br'], 'L0_ffn_Ws': _L0_ffn_in['Ws'], 'L0_ffn_bs': _L0_ffn_in['bs'], 'L0_ffn_Wo': _L0_ffn_in['Wo'], 'L0_ffn_bo': _L0_ffn_in['bo']}

def reference(x, L0_tok_W, L0_attn_W_Q, L0_attn_W_K, L0_attn_W_V, L0_ffn_route_id, L0_ffn_Wi, L0_ffn_bi, L0_ffn_Wr, L0_ffn_br, L0_ffn_Ws, L0_ffn_bs, L0_ffn_Wo, L0_ffn_bo):
    import jax
    import jax.numpy as jnp

    def _L0_tok_ref(x, W):
        import jax, jax.numpy as jnp
        import numpy as np
        PATCH_LEN = 16
        STRIDE = 8
        PAD = 8
        B, C, T, V = x.shape
        xp = jnp.pad(x, ((0, 0), (0, 0), (0, PAD), (0, 0)), mode='edge')
        Tp = T + PAD
        N = (Tp - PATCH_LEN) // STRIDE + 1
        idx = jnp.arange(N)[:, None] * STRIDE + jnp.arange(PATCH_LEN)[None, :]
        patches = xp[:, :, idx, :]
        patches = jnp.transpose(patches, (0, 4, 2, 3, 1))
        xf = jnp.fft.rfft(patches, axis=-2, norm='ortho')
        F = xf.shape[-2]
        x_real = xf.real.reshape(B, V, N, F * C)
        x_imag = xf.imag.reshape(B, V, N, F * C)
        x_emb = jnp.concatenate([x_real, x_imag], axis=-1)
        x_emb = x_emb @ W.T
        return x_emb.reshape(B, V * N, -1)

    def _L0_attn_ref(X, W_Q, W_K, W_V):
        import jax, jax.numpy as jnp
        import numpy as np
        GAMMA = 0.96875
        ROPE_THETA = 10000.0

        def _rope(x):
            B, S, d = x.shape
            inv_freq = 1.0 / ROPE_THETA ** (jnp.arange(0, d, 2, dtype=jnp.float32) / d)
            angles = jnp.arange(S, dtype=jnp.float32)[:, None] * inv_freq[None, :]
            cos = jnp.cos(angles).astype(x.dtype)
            sin = jnp.sin(angles).astype(x.dtype)
            xs = x.reshape(B, S, d // 2, 2)
            x0, x1 = (xs[..., 0], xs[..., 1])
            out = jnp.stack([x0 * cos - x1 * sin, x1 * cos + x0 * sin], axis=-1)
            return out.reshape(B, S, d)

        def _decay_mask(S, dtype):
            n = jnp.arange(S)[:, None]
            m = jnp.arange(S)[None, :]
            diff = n - m
            D = jnp.exp(jnp.maximum(diff, 0).astype(jnp.float32) * np.log(GAMMA))
            return jnp.where(diff >= 0, D, 0.0).astype(dtype)
        B, S, _ = X.shape
        D = _decay_mask(S, X.dtype)
        Q = _rope(X @ W_Q)
        K = _rope(X @ W_K)
        V = X @ W_V
        ret = jnp.einsum('bqd,bkd->bqk', Q, K) * D[None]
        return ret @ V

    def _L0_ffn_ref(x, route_id, Wi, bi, Wr, br, Ws, bs, Wo, bo):
        import jax, jax.numpy as jnp
        import numpy as np
        B, T, IN_DIM = (64, 64, 64)
        HID, OUT_DIM = (128, 64)
        N_LAYERS, N_EXPERTS, N_SHARED = (2, 16, 1)
        flat = x.reshape(-1, x.shape[-1])
        n_tok = flat.shape[0]
        route = jnp.repeat(route_id, n_tok // route_id.shape[0])
        h = jax.nn.relu(flat @ Wi.T + bi)
        n_layers, n_experts = (Wr.shape[0], Wr.shape[1])
        for l in range(n_layers):
            shared = (jnp.einsum('nd,shd->snh', h, Ws[l]) + bs[l][:, None, :]).mean(axis=0)
            routed = jnp.zeros_like(h)
            for e in range(n_experts):
                ye = h @ Wr[l, e].T + br[l, e]
                routed = routed + jnp.where((route == e)[:, None], ye, 0.0)
            h = jax.nn.relu(shared + routed + h)
        out = h @ Wo.T + bo
        return out.reshape(*x.shape[:-1], out.shape[-1])
    h = _L0_tok_ref(x, L0_tok_W)
    h = _layernorm(h + _L0_attn_ref(h, L0_attn_W_Q, L0_attn_W_K, L0_attn_W_V), axis=-1)
    h = _layernorm(h + _L0_ffn_ref(h, L0_ffn_route_id, L0_ffn_Wi, L0_ffn_bi, L0_ffn_Wr, L0_ffn_br, L0_ffn_Ws, L0_ffn_bs, L0_ffn_Wo, L0_ffn_bo), axis=-1)
    return h

_drawn_inputs = setup_inputs


def setup_inputs(seed=0):
    import zlib

    import numpy as np

    out = dict(_drawn_inputs(seed))
    spreads = {'L0_ffn_bi': (0.0, 0.499), 'L0_ffn_bo': (0.0, 0.1)}
    factors = {'L0_attn_W_Q': 3.063,
     'L0_attn_W_K': 3.012,
     'L0_attn_W_V': 3.0,
     'L0_ffn_Wi': 2.684,
     'L0_ffn_Wr': 7.03,
     'L0_ffn_br': 8.0,
     'L0_ffn_Ws': 7.127,
     'L0_ffn_bs': 8.0}
    for name, (base, spread) in spreads.items():
        noise = np.random.default_rng([zlib.crc32(name.encode()), seed]).standard_normal(out[name].shape)
        drawn = base * np.exp(spread * noise) if base else spread * noise
        out[name] = jnp.asarray(drawn.astype(out[name].dtype))
    for name, factor in factors.items():
        out[name] = (out[name] * factor).astype(out[name].dtype)
    return out
```

```python
from contextlib import ExitStack

import numpy as np
import concourse.bass as bass
from concourse import mybir

ALU = mybir.AluOpType
ACT = mybir.ActivationFunctionType
AX_X = mybir.AxisListType.X
F32 = mybir.dt.float32
I32 = mybir.dt.int32

B, C, T, V = 2, 64, 128, 64
PATCH, STRIDE = 16, 8
NPATCH = T // STRIDE
SEQ = V * NPATCH
RF = 2 * (PATCH // 2 + 1)
D = 64
OS = 4
OG = D // OS
QT4 = STRIDE // 2
CH = 128
NCH = SEQ // CH
UC = 4
UT = UC * CH
NU = B * SEQ // UT
HID = 128
NL, NE = 2, 16
NG = 64
GT = B * SEQ // NG
UG = UT // GT
GAMMA = 0.96875
THETA = 10000.0
EPS = 1e-5
STATE_DECAY = GAMMA ** CH


def constants():
    f = np.arange(PATCH // 2 + 1)[:, None] * np.arange(PATCH)[None, :] * (2 * np.pi / PATCH)
    dft = np.concatenate([np.cos(f), -np.sin(f)]) / np.sqrt(PATCH)
    dft_blocks = np.zeros((OS, RF, OS, PATCH))
    for s in range(OS):
        dft_blocks[s, :, s, :] = dft
    inv_freq = (1.0 / THETA ** (np.arange(0, D, 2, dtype=np.float32) / np.float32(D))).astype(np.float32)
    angle = (np.arange(SEQ, dtype=np.float32)[:, None] * inv_freq[None, :]).astype(np.float64)
    local = np.arange(SEQ) % CH
    decay = np.stack([GAMMA ** (local + 1.0), GAMMA ** (CH - 1.0 - local)], 1)
    cos = decay[:, :, None, None] * np.cos(angle)[:, None, :, None] * np.ones(2)
    sin = decay[:, :, None, None] * np.sin(angle)[:, None, :, None] * np.array([-1.0, 1.0])
    rope = np.stack([cos, sin]).reshape(2, NCH, CH, 2 * D).transpose(2, 0, 1, 3)
    key, query = np.arange(CH)[:, None], np.arange(CH)[None, :]
    mask = np.where(query >= key, GAMMA ** -float(CH), 0.0)
    center = np.eye(D) - 1.0 / D
    f32 = lambda a: np.ascontiguousarray(a, np.float32)
    return {
        "dft_blocks": f32(dft_blocks.reshape(OS * RF, OS * PATCH)),
        "rope": f32(rope),
        "mask_identity": f32(np.concatenate([mask, np.eye(CH)], 1)),
        "center2": f32(np.concatenate([center, center])),
        "expert_ids": f32(np.arange(NE)[:, None]),
    }


def build(nc, x, w_tok, w_qk, w_vT, route, w_inT, b_in, w_routedT, b_routed, w_sharedT, b_shared,
          w_out, b_out, dft_blocks, rope, mask_identity, center2, expert_ids, out):
    with ExitStack() as ctx:
        def sb(name, shape, dt=F32):
            return ctx.enter_context(nc.sbuf_tensor(name, shape, dt))

        def sem(name):
            return ctx.enter_context(nc.semaphore(name))

        bank = [ctx.enter_context(nc.psum_tensor(f"bank{i}", [128, 512], F32)) for i in range(8)]

        x_sb = sb("x_sb", [128, B, NPATCH, QT4, V])
        wtok_sb = sb("wtok_sb", [OS * RF, OG, 2 * C])
        dft_sb = sb("dft_sb", [OS * RF, OS * PATCH])
        wqkv = sb("wqkv", [128, 3 * D])
        wvT_sb = sb("wvT_sb", [D, 2, D])
        center_sb = sb("center_sb", [128, D])
        maskid = sb("maskid", [128, 2 * CH])
        rope_sb = sb("rope_sb", [128, 2, NCH, 2 * D])
        win_sb = sb("win_sb", [D, HID])
        bin_sb = sb("bin_sb", [HID, 1])
        wsh_sb = sb("wsh_sb", [HID, NL, HID])
        bsh_sb = sb("bsh_sb", [HID, NL])
        br_sb = sb("br_sb", [NE, NL, HID])
        wo_sb = sb("wo_sb", [D, HID])
        id_bo = sb("id_bo", [D, D + 1])
        route_sb = sb("route_sb", [NE, NG], I32)
        ids_sb = sb("ids_sb", [NE, 1])
        wroute = sb("wroute", [HID, NG, NL, HID])
        mask = maskid[:, 0:CH]
        ident = maskid[:, CH:2 * CH]

        weff = sb("weff", [128, QT4 + 1, 2, D])
        y_sb = sb("y_sb", [128, B, V, NPATCH])
        qk = sb("qk", [128, NU, UC, 2 * D])
        rope_tmp = sb("rope_tmp", [128, 2, UC, 2 * D])
        v_sb = sb("v_sb", [128, NU, UC, D])
        qT = sb("qT", [D, 2, UC, CH])
        kT = sb("kT", [D, 2, UC, CH])
        sT = sb("sT", [128, 2, UC, CH])
        state = sb("state", [D, B * NCH, D])
        sq = sb("sq", [128, 2, UC, D])
        stat = sb("stat", [128, 2 * NU, 3, UC])
        h1 = sb("h1", [128, NU, UC, D])
        h1T = sb("h1T", [D + 1, NU, UT])
        hid = sb("hid", [HID, NL + 1, 2, UT])
        res = sb("res", [128, NU, UC, D])
        onehot = sb("onehot", [NE, NG])
        route_f = sb("route_f", [NE, NG])
        bias = sb("bias", [HID, NL, NG])
        wo_c = sb("wo_c", [HID, D])
        cbo = sb("cbo", [D + 1, D])

        wtok_in, x_in = sem("wtok_in"), [sem(f"x_in{i}") for i in range(NU)]
        small_in, rope_in, ffn_in, route_in = sem("small_in"), sem("rope_in"), sem("ffn_in"), sem("route_in")
        gathered = [sem(f"gathered{u}") for u in range(NU)]
        stored = sem("stored")
        weff_mm, setup_mm, tok_mm, pad_mm = sem("weff_mm"), sem("setup_mm"), sem("tok_mm"), sem("pad_mm")
        proj_mm, qkT_mm, score_mm, state_mm = sem("proj_mm"), sem("qkT_mm"), sem("score_mm"), sem("state_mm")
        o_mm, h1T_mm, in_mm, l_mm, out_mm = sem("o_mm"), sem("h1T_mm"), sem("in_mm"), sem("l_mm"), sem("out_mm")
        weff_dve, weff_act, pad_zero, onehot_done = sem("weff_dve"), sem("weff_act"), sem("pad_zero"), sem("onehot_done")
        wres_done, setup_dve, setup_act = sem("wres_done"), sem("setup_dve"), sem("setup_act")
        y_lo, y_hi, y_pad = sem("y_lo"), sem("y_hi"), sem("y_pad")
        rope_parts, rope_done, v_done, qT_done, kT_done = (sem("rope_parts"), sem("rope_done"), sem("v_done"),
                                                           sem("qT_done"), sem("kT_done"))
        masked, state_done = sem("masked"), sem("state_done")
        sq_done, ms_done, eps_done, sd_done, rstd_done, ln_done = (sem("sq_done"), sem("ms_done"), sem("eps_done"), sem("sd_done"),
                                                         sem("rstd_done"), sem("ln_done"))
        h1T_done, in_done, biased, relu_done, ones_done, dve_setup = (sem("h1T_done"), sem("in_done"), sem("biased"),
                                                           sem("relu_done"), sem("ones_done"), sem("dve_setup"))

        tok_bank = [bank[0], bank[1], bank[6], bank[7]]
        pad_ps = bank[5][:, 0:B * V].rearrange("p (b v) -> p b v", b=B)
        qk_ps = bank[2][:, :].rearrange("p (c d) -> p c d", c=UC)
        v_ps = bank[3][:, 0:UC * D].rearrange("p (c d) -> p c d", c=UC)
        h1T_ps = bank[3]
        qkT_ps = bank[4]
        sT_ps = bank[5][:, :].rearrange("p (c n) -> p c n", c=UC)
        state_ps = bank[6][0:D, 0:UC * D].rearrange("p (c d) -> p c d", c=UC)
        ln_ps = bank[7][:, 0:UC * D].rearrange("p (c d) -> p c d", c=UC)
        wvc_ps, woc_ps = bank[4][:, 0:D], bank[4][:, D:2 * D]
        cbo_ps = bank[4][0:D + 1, 2 * D:3 * D]
        bias_ps = bank[4][:, 3 * D:3 * D + NL * NG].rearrange("p (l g) -> p l g", l=NL)

        def ff_use(kind, u):
            order = [(k, s - 5 - k) for s in range(NU + 8) for k in (2, 1, 0) if 0 <= s - 5 - k < NU]
            return order.index((kind, u))

        def ff_bank(kind, u):
            return bank[ff_use(kind, u) % 2]

        def layer_turn(k, u):
            order = [(kk, s - 5 - kk) for s in range(NU + 8) for kk in (2, 1) if 0 <= s - 5 - kk < NU]
            return order.index((k, u)) + 1

        def states_before(u):
            return (u // 2) * (NCH - 1) + (u % 2) * UC

        def unit(u):
            return u // 2, u % 2

        def wave(stages):
            for s in range(NU + len(stages) - 1):
                for k in reversed(range(len(stages))):
                    if stages[k] and 0 <= s - k < NU:
                        stages[k](s - k)

        block = ctx.enter_context(nc.Block())

        @block.sync
        def _(sp):
            xv = x.rearrange("b c (k q u) v -> b q c k (u v)", k=NPATCH, q=2)

            def load_x(u, parts):
                b, half = unit(u)
                k = NPATCH // 2
                for n in range(parts):
                    k0, k1 = half * k + n * k // parts, half * k + (n + 1) * k // parts
                    for q in range(2):
                        dst = x_sb[q * C:(q + 1) * C, b, k0:k1, :, :].rearrange("p k u v -> p k (u v)")
                        sp.dma_start(dst, xv[b, q, :, k0:k1, :]).then_inc(x_in[u], 16)

            sp.dma_start(wtok_sb[:, :, :], w_tok).then_inc(wtok_in, 16)
            sp.dma_start(dft_sb[:, :], dft_blocks).then_inc(wtok_in, 16)
            for u in range(NU):
                load_x(u, 1)
            sp.wait_ge(route_in, 16)
            for u in range(NU):
                with sp.Fori(0, UG) as g:
                    e = sp.value_load(route_sb[0:1, bass.ds(g + u * UG, 1)], min_val=0, max_val=NE - 1)
                    sp.dma_start(wroute[:, bass.ds(g + u * UG, 1), :, :].rearrange("p g l h -> p (g l h)"),
                                 w_routedT[bass.ds(e, 1), :, :].rearrange("e p n -> p (e n)")).then_inc(gathered[u], 16)
            ov = out.rearrange("b (c p) d -> b p c d", p=CH)
            for u in range(NU):
                b, half = unit(u)
                sp.wait_ge(ln_done, NU + u + 1)
                sp.dma_start(ov[b, :, half * UC:(half + 1) * UC, :], res[:, u, :, :]).then_inc(stored, 16)
            sp.wait_ge(stored, 16 * NU)

        @block.gpsimd
        def _(pool):
            pool.dma_start(wqkv[0:C, 0:2 * D], w_qk).then_inc(small_in, 16)
            pool.dma_start(wqkv[C:128, 0:2 * D], w_qk).then_inc(small_in, 16)
            for q in range(2):
                pool.dma_start(wvT_sb[:, q, :], w_vT).then_inc(small_in, 16)
            pool.dma_start(center_sb[:, :], center2).then_inc(small_in, 16)
            pool.dma_start(maskid[:, :], mask_identity).then_inc(small_in, 16)
            pool.dma_start(route_sb[:, :], route.partition_broadcast(NE)).then_inc(route_in, 16)
            pool.dma_start(ids_sb[:, :], expert_ids).then_inc(ffn_in, 16)
            pool.dma_start(br_sb[:, :, :], b_routed.rearrange("l e h -> e l h")).then_inc(ffn_in, 16)
            pool.dma_start(bsh_sb[:, :], b_shared).then_inc(ffn_in, 16)
            pool.dma_start(wo_sb[:, :], w_out).then_inc(ffn_in, 16)
            pool.dma_start(id_bo[:, 0:D], mask_identity[0:D, CH:CH + D]).then_inc(ffn_in, 16)
            pool.dma_start(id_bo[:, D:D + 1], b_out).then_inc(ffn_in, 16)
            pool.dma_start(wsh_sb[:, :, :], w_sharedT.rearrange("l d h -> d l h")).then_inc(ffn_in, 16)
            pool.dma_start(win_sb[:, :], w_inT).then_inc(ffn_in, 16)
            pool.dma_start(bin_sb[:, :], b_in).then_inc(ffn_in, 16)
            pool.dma_start(rope_sb[:, :, :, :], rope).then_inc(rope_in, 16)

        FFN_LOADS = 9 * 16
        SMALL_LOADS = 6 * 16

        @block.tensor
        def _(pe):
            mm = nc.tensor.matmul

            pe.wait_ge(wtok_in, 32)
            for g in range(OG):
                last = mm(bank[2 + g // 8][:, (g % 8) * 64:(g % 8 + 1) * 64], wtok_sb[:, g, :], dft_sb[:, :], start=True, stop=True)
            last.then_inc(weff_mm, 1)
            pe.wait_ge(small_in, SMALL_LOADS)
            pe.wait_ge(ffn_in, FFN_LOADS)
            pe.wait_ge(onehot_done, 1)
            mm(wvc_ps, wvT_sb[:, :, :].rearrange("p q d -> p (q d)"), center_sb[0:D, :], start=True, stop=True)
            mm(woc_ps, wo_sb[:, :], center_sb[0:D, :], start=True, stop=True)
            mm(cbo_ps, id_bo[:, :], center_sb[0:D, :], start=True, stop=True)
            for l in range(NL):
                last = mm(bias_ps[:, l, :], br_sb[:, l, :], onehot[:, :], start=True, stop=True)
            last.then_inc(setup_mm, 1)

            def tokenize(t):
                b, half = unit(t)
                k = NPATCH // 2
                pe.wait_ge(x_in[t], 32)
                for u in range(QT4):
                    last = mm(tok_bank[t][:, :], weff[:, u, :, :].rearrange("p h o -> p (h o)"),
                              x_sb[:, b, half * k:(half + 1) * k, u, :], start=(u == 0), stop=(u == QT4 - 1))
                last.then_inc(tok_mm, 1)

            def pad(b):
                if b:
                    pe.wait_ge(y_pad, b)
                mm(pad_ps[:, b, :], weff[:, QT4, :, :].rearrange("p h o -> p (h o)"),
                   x_sb[:, b, NPATCH - 1, QT4 - 1, :], start=True, stop=True).then_inc(pad_mm, 1)

            def project(u):
                b, half = unit(u)
                pe.wait_ge(y_lo, 2 * b + 2)
                pe.wait_ge(y_hi, 2 * b + 2)
                pe.wait_ge(y_pad, b + 1)
                if u:
                    pe.wait_ge(rope_parts, 2 * u)
                    pe.wait_ge(v_done, u)
                else:
                    pe.wait_ge(setup_act, 1)
                for c in range(UC):
                    yc = y_chunk(b, half * UC + c)
                    mm(qk_ps[:, c, :], yc, wqkv[:, 0:2 * D], start=True, stop=True)
                    last = mm(v_ps[:, c, :], yc, wqkv[:, 2 * D:3 * D], start=True, stop=True)
                last.then_inc(proj_mm, 1)

            def y_chunk(b, i):
                nv = CH // NPATCH
                return y_sb[:, b, i * nv:(i + 1) * nv, :].rearrange("p v n -> p (v n)")

            def transpose_qk(u):
                pe.wait_ge(rope_done, u + 1)
                if u:
                    pe.wait_ge(qT_done, u)
                    pe.wait_ge(kT_done, u)
                else:
                    pe.wait_ge(setup_dve, 3)
                for c in range(UC):
                    last = nc.tensor.transpose(qkT_ps[:, c * CH:(c + 1) * CH], qk[:, u, c, :], ident)
                last.then_inc(qkT_mm, 1)

            def scores(u):
                b, half = unit(u)
                pe.wait_ge(qT_done, u + 1)
                pe.wait_ge(kT_done, u + 1)
                if u:
                    pe.wait_ge(masked, u)
                else:
                    pe.wait_ge(y_pad, B)
                for c in range(UC):
                    last = mm(sT_ps[:, c, :], kT[:, u % 2, c, :], qT[:, u % 2, c, :], start=True, stop=True)
                last.then_inc(score_mm, 1)
                pe.wait_ge(v_done, u + 1)
                if u:
                    pe.wait_ge(state_done, states_before(u))
                else:
                    pe.wait_ge(y_lo, 3)
                    pe.wait_ge(y_hi, 3)
                for c in range(UC - half):
                    last = mm(state_ps[:, c, :], qk[:, u, c, D:2 * D], v_sb[:, u, c, :], start=True, stop=True)
                last.then_inc(state_mm, 1)

            def retention(u):
                b, half = unit(u)
                pe.wait_ge(masked, u + 1)
                if u:
                    pe.wait_ge(ln_done, u)
                else:
                    pe.wait_ge(y_lo, 4)
                    pe.wait_ge(y_hi, 4)
                for c in range(UC):
                    i = half * UC + c
                    last = mm(ln_ps[:, c, :], y_chunk(b, i), center_sb[:, :], start=True, stop=False)
                    if i:
                        pe.wait_ge(state_done, states_before(u) + c)
                        mm(ln_ps[:, c, :], qT[:, u % 2, c, :], state[:, b * NCH + i - 1, :], start=False, stop=False)
                    last = mm(ln_ps[:, c, :], sT[:, u % 2, c, :], v_sb[:, u, c, :], start=False, stop=True)
                last.then_inc(o_mm, 1)

            def transpose_h1(u):
                pe.wait_ge(ln_done, u + 1)
                pe.wait_ge(v_done, min(NU, u + 4))
                if u:
                    pe.wait_ge(h1T_done, u)
                for c in range(UC):
                    last = nc.tensor.transpose(h1T_ps[0:D, c * CH:(c + 1) * CH], h1[:, u, c, :], ident)
                last.then_inc(h1T_mm, 1)

            def ff_bank_free(kind, u):
                n = ff_use(kind, u) - 2
                for k2 in range(3):
                    for u2 in range(NU):
                        if n >= 0 and ff_use(k2, u2) == n:
                            if k2 == 0:
                                pe.wait_ge(in_done, u2 + 1)
                            else:
                                pe.wait_ge(biased, layer_turn(k2, u2))

            def ffn_in_proj(u):
                pe.wait_ge(h1T_done, u + 1)
                if u == 0:
                    pe.wait_ge(ffn_in, FFN_LOADS)
                ff_bank_free(0, u)
                mm(ff_bank(0, u)[:, :], win_sb[:, :], h1T[0:D, u, :], start=True, stop=True).then_inc(in_mm, 1)

            def ffn_layer(l):
                def run(u):
                    if l == 0:
                        pe.wait_ge(in_done, u + 1)
                        pe.wait_ge(gathered[u], 16 * UG)
                        if u == 0:
                            pe.wait_ge(wres_done, 1)
                    else:
                        pe.wait_ge(relu_done, layer_turn(l, u))
                    ff_bank_free(1 + l, u)
                    ps = ff_bank(1 + l, u)
                    mm(ps[:, :], wsh_sb[:, l, :], hid[:, l, u % 2, :], start=True, stop=False)
                    for g in range(UG):
                        last = mm(ps[:, g * GT:(g + 1) * GT], wroute[:, u * UG + g, l, :],
                                  hid[:, l, u % 2, g * GT:(g + 1) * GT], start=False, stop=(g == UG - 1))
                    last.then_inc(l_mm, 1)
                return run

            def ffn_out(u):
                pe.wait_ge(relu_done, layer_turn(2, u))
                pe.wait_ge(ln_done, NU + u)
                for c in range(UC):
                    mm(ln_ps[:, c, :], h1T[:, u, c * CH:(c + 1) * CH], cbo[:, :], start=True, stop=False)
                    last = mm(ln_ps[:, c, :], hid[:, NL, u % 2, c * CH:(c + 1) * CH], wo_c[:, :],
                              start=False, stop=True)
                last.then_inc(out_mm, 1)

            pe.wait_ge(weff_dve, 4)
            pe.wait_ge(weff_act, 2)
            tokenize(0)
            tokenize(1)
            pad(0)
            tokenize(2)
            stages = [project, transpose_qk, scores, retention, transpose_h1, ffn_in_proj,
                      ffn_layer(0), ffn_layer(1), ffn_out]
            project(0)
            tokenize(3)
            pad(1)
            wave([lambda u: project(u) if u else None] + stages[1:])

        @block.vector
        def _(dve):
            ve = nc.vector
            ve.memset(weff[:, QT4, :, :], 0.0).then_inc(pad_zero, 1)
            ve.memset(h1T[D:D + 1, :, :], 1.0).then_inc(ones_done, 1)
            dve.wait_ge(weff_mm, 1)
            for k in range(2):
                src = bank[2 + k][0:C, :].rearrange("p (o h r) -> p r h o", h=2, r=STRIDE)
                ve.tensor_copy(weff[0:C, 0:QT4, 0, 32 * k:32 * k + 32], src[:, 0:QT4, 0, :]).then_inc(weff_dve, 1)
                ve.tensor_copy(weff[0:C, 0:QT4, 1, 32 * k:32 * k + 32], src[:, 0:QT4, 1, :]).then_inc(weff_dve, 1)
            dve.wait_ge(weff_act, 2)
            dve.wait_ge(pad_zero, 1)
            for k in range(2):
                src = bank[2 + k][C:128, :].rearrange("p (o h r) -> p o h r", h=2, r=STRIDE)
                ve.tensor_reduce(weff[C:128, QT4, 1, 32 * k:32 * k + 32], src[:, :, 1, :], AX_X,
                                 ALU.add).then_inc(weff_dve, 1)
            dve.wait_ge(route_in, 16)
            ve.tensor_copy(route_f[:, :], route_sb[:, :]).then_inc(dve_setup, 1)
            dve.wait_ge(dve_setup, 1)
            dve.wait_ge(ffn_in, FFN_LOADS)
            ve.tensor_scalar(onehot[:, :], route_f[:, :], ids_sb[:, 0:1], None, ALU.is_equal).then_inc(onehot_done, 1)
            dve.wait_ge(small_in, SMALL_LOADS)
            ve.tensor_tensor(wsh_sb[:, :, :], wsh_sb[:, :, :], ident.unsqueeze(1).broadcast_to([128, NL, HID]),
                             ALU.add).then_inc(wres_done, 1)
            dve.wait_ge(setup_mm, 1)
            dve.wait_ge(setup_act, 1)
            ve.tensor_copy(wo_c[:, :], woc_ps).then_inc(setup_dve, 1)
            ve.tensor_copy(cbo[:, :], cbo_ps).then_inc(setup_dve, 1)
            ve.tensor_tensor(bias[:, :, :], bias_ps, bsh_sb[:, :].unsqueeze(2).broadcast_to([HID, NL, NG]),
                             ALU.add).then_inc(setup_dve, 1)

            def y_second(t):
                b, half = unit(t)
                k = NPATCH // 2
                dve.wait_ge(tok_mm, t + 1)
                src = tok_bank[t][C:128, :].rearrange("p (k v) -> p v k", k=k)
                if half:
                    ve.tensor_copy(y_sb[C:128, b, :, k - 1:2 * k - 1], src).then_inc(y_hi, 1)
                else:
                    ve.tensor_copy(y_sb[C:128, b, :, 0:k - 1], src[:, :, 1:k]).then_inc(y_hi, 1)

            def y_padding(b):
                dve.wait_ge(pad_mm, b + 1)
                ve.tensor_copy(y_sb[C:128, b, :, NPATCH - 1], pad_ps[C:128, b, :]).then_inc(y_pad, 1)

            def rotate(u):
                b, half = unit(u)
                cos = rope_sb[:, 0, half * UC:(half + 1) * UC, :]
                sin = rope_sb[:, 1, half * UC:(half + 1) * UC, :]
                dve.wait_ge(proj_mm, u + 1)
                if u == 0:
                    dve.wait_ge(rope_in, 16)
                ve.tensor_tensor(qk[:, u, :, :], qk_ps, cos, ALU.mult).then_inc(rope_parts, 1)
                if u >= 2:
                    dve.wait_ge(rope_done, u - 1)
                pairs = qk_ps.rearrange("p c (i two) -> p (c i) two", two=2)[:, :, ::-1]
                ve.tensor_tensor(rope_tmp[:, u % 2, :, :].rearrange("p c (i two) -> p (c i) two", two=2), pairs,
                                 sin.rearrange("p c (i two) -> p (c i) two", two=2), ALU.mult).then_inc(rope_parts, 1)
                dve.wait_ge(rope_parts, 2 * u + 2)
                ve.tensor_tensor(qk[:, u, :, :], qk[:, u, :, :], rope_tmp[:, u % 2, :, :],
                                 ALU.add).then_inc(rope_done, 1)

            def keys(u):
                dve.wait_ge(qkT_mm, u + 1)
                if u >= 2:
                    dve.wait_ge(score_mm, u - 1)
                ve.tensor_copy(kT[:, u % 2, :, :].rearrange("p c n -> p (c n)"),
                               qkT_ps[D:2 * D, :]).then_inc(kT_done, 1)

            def mask_scores(u):
                b, half = unit(u)
                dve.wait_ge(score_mm, u + 1)
                if u >= 2:
                    dve.wait_ge(o_mm, u - 1)
                ve.tensor_tensor(sT[:, u % 2, :, :], sT_ps, mask.unsqueeze(1).broadcast_to([128, UC, CH]),
                                 ALU.mult).then_inc(masked, 1)
                dve.wait_ge(state_mm, u + 1)
                for c in range(UC - half):
                    i = half * UC + c
                    s = b * NCH + i
                    if i == 0:
                        ve.tensor_copy(state[:, s, :], state_ps[:, c, :]).then_inc(state_done, 1)
                    else:
                        dve.wait_ge(state_done, states_before(u) + c)
                        ve.scalar_tensor_tensor(state[:, s, :], state[:, s - 1, :], STATE_DECAY, state_ps[:, c, :],
                                                ALU.mult, ALU.add).then_inc(state_done, 1)

            def layernorm(n, u, dst):
                k = n * NU + u
                dve.wait_ge(sq_done, k + 1)
                ve.tensor_reduce(stat[:, k, 0, :], sq[:, k % 2, :, :], AX_X, ALU.add).then_inc(ms_done, 1)
                dve.wait_ge(ms_done, k + 1)
                ve.tensor_scalar(stat[:, k, 0, :], stat[:, k, 0, :], EPS, None, ALU.add).then_inc(eps_done, 1)
                dve.wait_ge(sd_done, k + 1)
                ve.reciprocal(stat[:, k, 2, :], stat[:, k, 1, :]).then_inc(rstd_done, 1)
                dve.wait_ge(rstd_done, k + 1)
                ve.tensor_tensor(dst[:, u, :, :], ln_ps, stat[:, k, 2, :].unsqueeze(2).broadcast_to([128, UC, D]),
                                 ALU.mult).then_inc(ln_done, 1)

            def add_bias(l):
                def run(u):
                    n = layer_turn(1 + l, u)
                    dve.wait_ge(l_mm, n)
                    if l == 0 and u >= 2:
                        dve.wait_ge(l_mm, layer_turn(2, u - 2))
                    if l == 1 and u >= 2:
                        dve.wait_ge(out_mm, u - 1)
                    ps = ff_bank(1 + l, u)[:, :].rearrange("p (g t) -> p g t", g=UG)
                    b_g = bias[:, l, u * UG:(u + 1) * UG].unsqueeze(2).broadcast_to([HID, UG, GT])
                    ve.tensor_tensor(hid[:, 1 + l, u % 2, :].rearrange("p (g t) -> p g t", g=UG), ps, b_g,
                                     ALU.add).then_inc(biased, 1)
                return run

            y_second(0)
            y_second(1)
            y_padding(0)
            y_second(2)
            rotate(0)
            y_second(3)
            y_padding(1)
            wave([lambda u: rotate(u) if u else None, keys, mask_scores, lambda u: layernorm(0, u, h1), None, None,
                  add_bias(0), add_bias(1), lambda u: layernorm(1, u, res)])

        @block.scalar
        def _(act):
            se = nc.scalar
            act.wait_ge(weff_mm, 1)
            for k in range(2):
                src = bank[2 + k][C:128, :].rearrange("p (o h r) -> p r h o", h=2, r=STRIDE)
                for h in range(2):
                    ins = se.copy(weff[C:128, 0:QT4, h, 32 * k:32 * k + 32], src[:, QT4:2 * QT4, h, :])
                ins.then_inc(weff_act, 1)
            act.wait_ge(setup_mm, 1)
            se.copy(wqkv[:, 2 * D:3 * D], wvc_ps).then_inc(setup_act, 1)

            def y_first(t):
                b, half = unit(t)
                k = NPATCH // 2
                act.wait_ge(tok_mm, t + 1)
                se.copy(y_sb[0:C, b, :, half * k:(half + 1) * k],
                        tok_bank[t][0:C, :].rearrange("p (k v) -> p v k", k=k)).then_inc(y_lo, 1)

            def values(u):
                act.wait_ge(proj_mm, u + 1)
                se.copy(v_sb[:, u, :, :], v_ps).then_inc(v_done, 1)

            def queries(u):
                act.wait_ge(qkT_mm, u + 1)
                if u >= 2:
                    act.wait_ge(o_mm, u - 1)
                se.copy(qT[:, u % 2, :, :].rearrange("p c n -> p (c n)"), qkT_ps[0:D, :]).then_inc(qT_done, 1)

            def squares(n, ready):
                def run(u):
                    k = n * NU + u
                    act.wait_ge(ready, u + 1)
                    if k >= 2:
                        act.wait_ge(ms_done, k - 1)
                    se.activation(sq[:, k % 2, :, :], ln_ps, ACT.Square, scale=1.0 / D ** 0.5).then_inc(sq_done, 1)
                    act.wait_ge(eps_done, k + 1)
                    se.activation(stat[:, k, 1, :], stat[:, k, 0, :], ACT.Sqrt).then_inc(sd_done, 1)
                return run

            def copy_h1T(u):
                act.wait_ge(h1T_mm, u + 1)
                se.copy(h1T[0:D, u, :], h1T_ps[0:D, :]).then_inc(h1T_done, 1)

            def relu_in(u):
                act.wait_ge(in_mm, u + 1)
                if u >= 2:
                    act.wait_ge(l_mm, layer_turn(1, u - 2))
                se.activation(hid[:, 0, u % 2, :], ff_bank(0, u)[:, :], ACT.Relu, bias=bin_sb[:, 0:1]).then_inc(in_done, 1)

            def relu(l):
                def run(u):
                    act.wait_ge(biased, layer_turn(1 + l, u))
                    h = hid[:, 1 + l, u % 2, :]
                    se.activation(h, h, ACT.Relu).then_inc(relu_done, 1)
                return run

            y_first(0)
            y_first(1)
            y_first(2)
            values(0)
            y_first(3)
            act.wait_ge(ffn_in, FFN_LOADS)
            wave([lambda u: values(u) if u else None, queries, None, squares(0, o_mm), copy_h1T, relu_in,
                  relu(0), relu(1), squares(1, out_mm)])


def kernel(x, L0_tok_W, L0_attn_W_Q, L0_attn_W_K, L0_attn_W_V, L0_ffn_route_id, L0_ffn_Wi, L0_ffn_bi,
           L0_ffn_Wr, L0_ffn_br, L0_ffn_Ws, L0_ffn_bs, L0_ffn_Wo, L0_ffn_bo):
    import concourse.bacc as bacc
    from concourse.bass_utils import run_bass_kernel_spmd

    a = lambda t: np.asarray(t)
    arrays = {
        "x": a(x),
        "w_tok": np.tile(a(L0_tok_W).reshape(OG, OS, RF, C).transpose(1, 2, 0, 3).reshape(OS * RF, OG, C), 2),
        "w_qk": np.concatenate([a(L0_attn_W_Q), a(L0_attn_W_K)], 1),
        "w_vT": a(L0_attn_W_V).T,
        "route": a(L0_ffn_route_id),
        "w_inT": a(L0_ffn_Wi).T,
        "b_in": a(L0_ffn_bi).reshape(HID, 1),
        "w_routedT": a(L0_ffn_Wr).transpose(1, 3, 0, 2).reshape(NE, HID, NL * HID),
        "b_routed": a(L0_ffn_br),
        "w_sharedT": a(L0_ffn_Ws)[:, 0].transpose(0, 2, 1),
        "b_shared": a(L0_ffn_bs)[:, 0].T,
        "w_out": a(L0_ffn_Wo),
        "b_out": a(L0_ffn_bo).reshape(D, 1),
        **constants(),
    }
    arrays = {k: np.ascontiguousarray(v) for k, v in arrays.items()}
    nc = bacc.Bacc("TRN2", target_bir_lowering=False, num_devices=1)
    aps = {k: nc.dram_tensor(k, v.shape, mybir.dt.from_np(v.dtype), kind="ExternalInput").ap()
           for k, v in arrays.items()}
    aps["out"] = nc.dram_tensor("out", (B, SEQ, D), F32, kind="ExternalOutput").ap()
    build(nc, **aps)
    r = run_bass_kernel_spmd(nc, [arrays], core_ids=[0])
    return r.results[0]["out"]
```

```python
from contextlib import ExitStack

import numpy as np
import concourse.bass as bass
from concourse import mybir

ALU = mybir.AluOpType
ACT = mybir.ActivationFunctionType
AX_X = mybir.AxisListType.X
F32 = mybir.dt.float32
I32 = mybir.dt.int32

B, C, T, V = 2, 64, 128, 64
PATCH, STRIDE = 16, 8
NPATCH = T // STRIDE
SEQ = V * NPATCH
RF = 2 * (PATCH // 2 + 1)
D = 64
OS = 4
OG = D // OS
TQ = STRIDE // 2
HB = NPATCH // 2
NT = 2 * B
CH = 128
NCH = SEQ // CH
UC = 2
UB = NCH // UC
NU = B * UB
UT = UC * CH
HID = 128
NL, NE = 2, 16
NG = 64
GT = B * SEQ // NG
CG = CH // GT
QTS = 4
UG = UC * CG
GAMMA = 0.96875
THETA = 10000.0
EPS = 1e-5
STATE_DECAY = GAMMA ** CH

PROJ, QKT, SCORE, RET, H1T, IN, L0, L0T, L1, L1T, OUT = range(11)
START = (0, 1, 2, 3, 4, 5, 6, 7)
RING = (IN, L0, L0T, L1, L1T)
LAYER = (L0, L1)
LAYER_T = (L0T, L1T)
NORMS = (RET, OUT)

PACKED = [("wqk", 2 * D), ("wvc", D), ("center", D), ("mask", CH), ("ident", CH), ("wsh", NL * HID),
          ("wvT", 2 * D), ("w_in", HID), ("w_out", HID), ("b_out", CH), ("b_in", 1), ("b_sh", NL),
          ("b_routed", NL * HID), ("expert_ids", 1)]


def packed_at(name):
    at = 0
    for n, w in PACKED:
        if n == name:
            return at, at + w
        at += w


def wave():
    return [(k, u) for s in range(START[-1] + OUT + 1) for k in range(OUT, -1, -1) for u in range(NU)
            if START[u] + k == s]


def turn(stages, k, u):
    runs = [x for x in wave() if x[0] in stages]
    return runs.index((k, u)) + 1


def ran(stage, k, u):
    runs = wave()
    return sum(x[0] == stage for x in runs[:runs.index((k, u))])


def constants():
    f = np.arange(PATCH // 2 + 1)[:, None] * np.arange(PATCH)[None, :] * (2 * np.pi / PATCH)
    dft = np.concatenate([np.cos(f), -np.sin(f)]) / np.sqrt(PATCH)
    dft_blocks = np.zeros((OS, RF, OS, PATCH))
    for s in range(OS):
        dft_blocks[s, :, s, :] = dft
    inv_freq = (1.0 / THETA ** (np.arange(0, D, 2, dtype=np.float32) / np.float32(D))).astype(np.float32)
    angle = (np.arange(SEQ, dtype=np.float32)[:, None] * inv_freq[None, :]).astype(np.float64)
    local = np.arange(SEQ) % CH
    decay = np.stack([GAMMA ** (local + 1.0), GAMMA ** (CH - 1.0 - local)], 1)
    cos = decay[:, :, None, None] * np.cos(angle)[:, None, :, None] * np.ones(2)
    sin = decay[:, :, None, None] * np.sin(angle)[:, None, :, None] * np.array([-1.0, 1.0])
    rope = np.stack([cos, sin]).reshape(2, NCH, CH, 2 * D).transpose(2, 0, 1, 3)
    key, query = np.arange(CH)[:, None], np.arange(CH)[None, :]
    center = np.eye(D) - 1.0 / D
    f32 = lambda a: np.ascontiguousarray(a, np.float32)
    return {
        "dft": f32(dft_blocks.reshape(OS * RF, OS * PATCH)),
        "rope": f32(rope),
        "mask": f32(np.where(query >= key, GAMMA ** -float(CH), 0.0)),
        "ident": f32(np.eye(CH)),
        "center": f32(np.concatenate([center, center])),
        "expert_ids": f32(np.arange(NE)[:, None]),
    }


def build(nc, x, w_tok, small, route, w_routedT, rope, out):
    with ExitStack() as ctx:
        def sb(name, shape, dt=F32):
            return ctx.enter_context(nc.sbuf_tensor(name, shape, dt))

        def sem(name):
            return ctx.enter_context(nc.semaphore(name))

        bank = [ctx.enter_context(nc.psum_tensor(f"bank{i}", [128, 512], F32)) for i in range(8)]

        x_sb = sb("x_sb", [128, B, NPATCH, TQ, V])
        wtok_sb = sb("wtok_sb", [OS * RF, OS * PATCH + OG * C])
        small_sb = sb("small_sb", [128, packed_at("expert_ids")[1]])
        rope_sb = sb("rope_sb", [128, 2, NCH, 2 * D])
        route_sb = sb("route_sb", [NE, NG], I32)
        wroute = sb("wroute", [HID, NG, NL, HID])

        def packed(name, rows=128):
            a, b = packed_at(name)
            return small_sb[0:rows, a:b]

        mask, ident = packed("mask"), packed("ident")
        w_qk = packed("wqk")
        w_vh = small_sb[:, packed_at("wvc")[0]:packed_at("center")[1]]

        weff = sb("weff", [128, TQ + 1, 2, D])
        y_sb = sb("y_sb", [128, B, V, NPATCH])
        qk = sb("qk", [128, NU, UC, 2 * D])
        rope_tmp = sb("rope_tmp", [128, 2, UC, 2 * D])
        vh = sb("vh", [128, NU, UC, 2 * D])
        qT = sb("qT", [D, QTS, UT])
        kT = sb("kT", [D, 2, UT])
        sT = sb("sT", [128, 2, UC, CH])
        state = sb("state", [D, B * NCH, D])
        hsum = sb("hsum", [128, 2, UC, D])
        sq = sb("sq", [128, 2, UC, D])
        stat = sb("stat", [128, 2 * NU, 3, UC])
        h1 = sb("h1", [128, NU, UC, D])
        h1b = sb("h1b", [128, NU, UC, D])
        h1T = sb("h1T", [D, 2, UT])
        z = sb("z", [128, NL, 2, UC, HID])
        hid = sb("hid", [HID, NL + 1, 2, UT])
        res = sb("res", [128, NU, UC, D])
        eps_sb = sb("eps_sb", [128, 1])
        onehot = sb("onehot", [NE, NG])
        route_f = sb("route_f", [NE, NG])
        bias = sb("bias", [HID, NL, NG])
        wres = sb("wres", [HID, NL, HID])
        wo_c = sb("wo_c", [HID, D])
        bo_c = sb("bo_c", [128, D])

        wtok_in, x_in = sem("wtok_in"), [sem(f"x_in{i}") for i in range(NT)]
        small_in, rope_in, route_in = sem("small_in"), sem("rope_in"), sem("route_in")
        gathered = [sem(f"gathered{u}") for u in range(NU)]
        stored = sem("stored")
        weff_mm, setup_mm, tok_mm, pad_mm = sem("weff_mm"), sem("setup_mm"), sem("tok_mm"), sem("pad_mm")
        qk_mm, vh_mm, qkT_mm, score_mm = sem("qk_mm"), sem("vh_mm"), sem("qkT_mm"), sem("score_mm")
        norm_mm, h1T_mm, in_mm, layer_mm, layerT_mm = (sem("norm_mm"), sem("h1T_mm"), sem("in_mm"), sem("layer_mm"),
                                                       sem("layerT_mm"))
        weff_done, weff_act, pad_zero, pad_sum = sem("weff_done"), sem("weff_act"), sem("pad_zero"), sem("pad_sum")
        route_cast, onehot_done, wres_done = sem("route_cast"), sem("onehot_done"), sem("wres_done")
        wvc_done, setup_done = sem("wvc_done"), sem("setup_done")
        y_first, y_second, y_pad = sem("y_first"), sem("y_second"), sem("y_pad")
        rope_parts, rope_done, vh_done = sem("rope_parts"), sem("rope_done"), sem("vh_done")
        qT_done, kT_done, masked, state_done = sem("qT_done"), sem("kT_done"), sem("masked"), sem("state_done")
        sum_done, var_done, eps_set = sem("sum_done"), sem("var_done"), sem("eps_set")
        sd_done, rstd_done, norm_done, h1b_done = sem("sd_done"), sem("rstd_done"), sem("norm_done"), sem("h1b_done")
        h1T_done, in_done, z_done, biased, relu_done = (sem("h1T_done"), sem("in_done"), sem("z_done"), sem("biased"),
                                                        sem("relu_done"))

        tok_bank = [bank[0], bank[1], bank[6], bank[7]]
        pad_ps = bank[5][:, 0:B * V].rearrange("p (b v) -> p b v", b=B)
        qk_ps = bank[2][:, 0:UC * 2 * D].rearrange("p (c d) -> p c d", c=UC)
        vh_ps = bank[3][:, 0:UC * 2 * D].rearrange("p (c d) -> p c d", c=UC)
        qkT_ps = bank[4][:, 0:UT]
        h1T_ps = bank[4][0:D, UT:2 * UT]
        sT_ps = bank[5][:, 0:UT].rearrange("p (c n) -> p c n", c=UC)
        state_ps = bank[5][0:D, UT:UT + UC * D].rearrange("p (c d) -> p c d", c=UC)
        norm_ps = bank[7][:, 0:UC * D].rearrange("p (c d) -> p c d", c=UC)
        ring_bank = [bank[0], bank[1], bank[6]]
        wvc_ps, woc_ps, boc_ps = bank[4][:, 0:D], bank[4][:, D:2 * D], bank[4][:, 2 * D:3 * D]
        bias_ps = bank[4][:, 3 * D:3 * D + NL * NG].rearrange("p (l g) -> p l g", l=NL)

        def ring(k, u):
            return ring_bank[turn(RING, k, u) % 3][:, 0:UT]

        def states_before(u):
            return (u // UB) * (NCH - 1) + (u % UB) * UC

        def y_chunk(u, c):
            v0 = (u % UB * UC + c) * CH // NPATCH
            return y_sb[:, u // UB, v0:v0 + CH // NPATCH, :].rearrange("p v n -> p (v n)")

        def has_state(u, c):
            return u % UB * UC + c < NCH - 1

        block = ctx.enter_context(nc.Block())

        @block.sync
        def _(sp):
            xv = x.rearrange("b c (k q u) v -> b q c k (u v)", k=NPATCH, q=2)
            sp.dma_start(wtok_sb[:, :], w_tok).then_inc(wtok_in, 16)
            for t in range(NT):
                b, k0 = t // 2, t % 2 * HB
                for q in range(2):
                    dst = x_sb[q * C:(q + 1) * C, b, k0:k0 + HB, :, :].rearrange("p k u v -> p k (u v)")
                    sp.dma_start(dst, xv[b, q, :, k0:k0 + HB, :]).then_inc(x_in[t], 16)
                if t == 1:
                    sp.dma_start(small_sb[:, :], small).then_inc(small_in, 16)
                if t == 2:
                    sp.dma_start(rope_sb[:, :, :, :], rope).then_inc(rope_in, 16)
            sp.wait_ge(route_in, 16)
            ids = [sp.alloc_register(f"expert{g}") for g in range(UG)]
            for u in range(NU):
                sp.load(ids, route_sb[0:1, u * UG:(u + 1) * UG])
                for g in range(UG):
                    e = sp.snap(ids[g], min_val=0, max_val=NE - 1)
                    sp.dma_start(wroute[:, u * UG + g, :, :].rearrange("p l h -> p (l h)"),
                                 w_routedT[bass.ds(e, 1), :, :].rearrange("e p n -> p (e n)")).then_inc(gathered[u], 16)
            ov = out.rearrange("b (s c p) d -> (b s) p c d", c=UC, p=CH)
            for u in range(NU):
                sp.wait_ge(norm_done, turn(NORMS, OUT, u))
                sp.dma_start(ov[u], res[:, u, :, :]).then_inc(stored, 16)
            sp.wait_ge(stored, 16 * NU)

        @block.gpsimd
        def _(pool):
            pool.dma_start(route_sb[:, :], route.partition_broadcast(NE)).then_inc(route_in, 16)
            pool.wait_ge(setup_done, 3)
            for u in range(NU):
                pool.wait_ge(norm_done, turn(NORMS, RET, u))
                nc.gpsimd.tensor_tensor(h1b[:, u, :, :], h1[:, u, :, :],
                                        bo_c[:, :].unsqueeze(1).broadcast_to([128, UC, D]), ALU.add).then_inc(h1b_done, 1)

        @block.tensor
        def _(pe):
            mm = nc.tensor.matmul

            pe.wait_ge(wtok_in, 16)
            for g in range(OG):
                w = wtok_sb[:, OS * PATCH + g * C:OS * PATCH + (g + 1) * C]
                last = mm(bank[2 + g // 8][0:C, (g % 8) * 64:(g % 8 + 1) * 64], w, wtok_sb[:, 0:OS * PATCH],
                          start=True, stop=True)
            last.then_inc(weff_mm, 1)

            def tokenize(t):
                b, k0 = t // 2, t % 2 * HB
                pe.wait_ge(x_in[t], 32)
                for u in range(TQ):
                    last = mm(tok_bank[t][:, :], weff[:, u, :, :].rearrange("p h o -> p (h o)"),
                              x_sb[:, b, k0:k0 + HB, u, :], start=(u == 0), stop=(u == TQ - 1))
                last.then_inc(tok_mm, 1)

            def pad(b):
                if b:
                    pe.wait_ge(y_pad, b)
                else:
                    pe.wait_ge(pad_sum, 2)
                mm(pad_ps[:, b, :], weff[:, TQ, :, :].rearrange("p h o -> p (h o)"),
                   x_sb[:, b, NPATCH - 1, TQ - 1, :], start=True, stop=True).then_inc(pad_mm, 1)

            def small_products():
                pe.wait_ge(small_in, 16)
                pe.wait_ge(onehot_done, 1)
                c1 = packed("center", D)
                mm(wvc_ps, packed("wvT", D), c1, start=True, stop=True)
                mm(woc_ps, packed("w_out", D), c1, start=True, stop=True)
                mm(boc_ps, packed("b_out", D), c1, start=True, stop=True)
                for l in range(NL):
                    last = mm(bias_ps[:, l, :], packed("b_routed", NE)[:, l * HID:(l + 1) * HID], onehot[:, :],
                              start=True, stop=True)
                last.then_inc(setup_mm, 1)

            def project(u):
                b = u // UB
                pe.wait_ge(y_first, 2 * b + 2)
                pe.wait_ge(y_second, 2 * b + 2)
                pe.wait_ge(y_pad, b + 1)
                if u:
                    pe.wait_ge(rope_parts, 2 * u)
                for c in range(UC):
                    last = mm(qk_ps[:, c, :], y_chunk(u, c), w_qk, start=True, stop=True)
                last.then_inc(qk_mm, 1)
                if u:
                    pe.wait_ge(vh_done, u)
                else:
                    pe.wait_ge(wvc_done, 1)
                for c in range(UC):
                    last = mm(vh_ps[:, c, :], y_chunk(u, c), w_vh, start=True, stop=True)
                last.then_inc(vh_mm, 1)

            def transpose_qk(u):
                pe.wait_ge(rope_done, u + 1)
                if u:
                    pe.wait_ge(qT_done, u)
                    pe.wait_ge(kT_done, u)
                else:
                    pe.wait_ge(setup_done, 3)
                if ran(H1T, QKT, u):
                    pe.wait_ge(h1T_done, ran(H1T, QKT, u))
                for c in range(UC):
                    last = nc.tensor.transpose(qkT_ps[:, c * CH:(c + 1) * CH], qk[:, u, c, :], ident)
                last.then_inc(qkT_mm, 1)

            def scores(u):
                pe.wait_ge(vh_done, u + 1)
                pe.wait_ge(qT_done, u + 1)
                pe.wait_ge(kT_done, u + 1)
                if u:
                    pe.wait_ge(masked, u)
                    pe.wait_ge(state_done, states_before(u))
                else:
                    pe.wait_ge(y_pad, B)
                for c in range(UC):
                    if has_state(u, c):
                        mm(state_ps[:, c, :], qk[:, u, c, D:2 * D], vh[:, u, c, 0:D], start=True, stop=True)
                for c in range(UC):
                    last = mm(sT_ps[:, c, :], kT[:, u % 2, c * CH:(c + 1) * CH], qT[:, u % QTS, c * CH:(c + 1) * CH],
                              start=True, stop=True)
                last.then_inc(score_mm, 1)

            def retention(u):
                pe.wait_ge(masked, u + 1)
                if u:
                    pe.wait_ge(sum_done, turn(NORMS, RET, u) - 1)
                else:
                    pe.wait_ge(y_first, NT)
                    pe.wait_ge(y_second, NT)
                for c in range(UC):
                    i = u % UB * UC + c
                    if i:
                        pe.wait_ge(state_done, states_before(u) + c)
                        mm(norm_ps[:, c, :], qT[:, u % QTS, c * CH:(c + 1) * CH], state[:, u // UB * NCH + i - 1, :],
                           start=True, stop=False)
                    last = mm(norm_ps[:, c, :], sT[:, u % 2, c, :], vh[:, u, c, 0:D], start=(i == 0), stop=True)
                last.then_inc(norm_mm, 1)

            def transpose_h1(u):
                pe.wait_ge(norm_done, turn(NORMS, RET, u))
                pe.wait_ge(qT_done, ran(QKT, H1T, u))
                pe.wait_ge(kT_done, ran(QKT, H1T, u))
                if u:
                    pe.wait_ge(h1T_done, u)
                for c in range(UC):
                    last = nc.tensor.transpose(h1T_ps[:, c * CH:(c + 1) * CH], h1[:, u, c, :], ident)
                last.then_inc(h1T_mm, 1)

            def ring_free(k, u):
                n = turn(RING, k, u)
                if n > 3:
                    k0, u0 = [run for run in wave() if run[0] in RING][n - 4]
                    if k0 == IN:
                        pe.wait_ge(in_done, u0 + 1)
                    elif k0 in LAYER:
                        pe.wait_ge(z_done, turn(LAYER, k0, u0))
                    else:
                        pe.wait_ge(biased, turn(LAYER_T, k0, u0))

            def ffn_in(u):
                pe.wait_ge(h1T_done, u + 1)
                ring_free(IN, u)
                mm(ring(IN, u), packed("w_in", D), h1T[:, u % 2, :], start=True, stop=True).then_inc(in_mm, 1)

            def layer(l, k, u):
                if l == 0:
                    pe.wait_ge(in_done, u + 1)
                    pe.wait_ge(gathered[u], 16 * UG)
                    if u == 0:
                        pe.wait_ge(wres_done, 1)
                else:
                    pe.wait_ge(relu_done, turn(LAYER_T, L0T, u))
                ring_free(k, u)
                for c in range(UC):
                    ps, h = ring(k, u)[:, c * HID:(c + 1) * HID], hid[:, l, u % 2, c * CH:(c + 1) * CH]
                    mm(ps, h, wres[:, l, :], start=True, stop=False, skip_group_check=True)
                    for j in range(CG):
                        rows = slice(j * GT, (j + 1) * GT)
                        last = mm(ps[rows, :], h[:, rows], wroute[:, u * UG + c * CG + j, l, :],
                                  start=False, stop=True, skip_group_check=True)
                last.then_inc(layer_mm, 1)

            def layer_transpose(l, k, u):
                pe.wait_ge(z_done, turn(LAYER, LAYER[l], u))
                ring_free(k, u)
                for c in range(UC):
                    last = nc.tensor.transpose(ring(k, u)[:, c * CH:(c + 1) * CH], z[:, l, u % 2, c, :], ident)
                last.then_inc(layerT_mm, 1)

            def ffn_out(u):
                pe.wait_ge(relu_done, turn(LAYER_T, L1T, u))
                pe.wait_ge(sum_done, turn(NORMS, OUT, u) - 1)
                for c in range(UC):
                    last = mm(norm_ps[:, c, :], hid[:, NL, u % 2, c * CH:(c + 1) * CH], wo_c[:, :],
                              start=True, stop=True)
                last.then_inc(norm_mm, 1)

            pe.wait_ge(weff_done, 2)
            pe.wait_ge(weff_act, 2)
            tokenize(0)
            tokenize(1)
            pad(0)
            small_products()
            tokenize(2)
            for k, u in wave():
                if (k, u) == (SCORE, 0):
                    tokenize(3)
                    pad(1)
                if k == PROJ:
                    project(u)
                elif k == QKT:
                    transpose_qk(u)
                elif k == SCORE:
                    scores(u)
                elif k == RET:
                    retention(u)
                elif k == H1T:
                    transpose_h1(u)
                elif k == IN:
                    ffn_in(u)
                elif k in LAYER:
                    layer(LAYER.index(k), k, u)
                elif k in LAYER_T:
                    layer_transpose(LAYER_T.index(k), k, u)
                else:
                    ffn_out(u)

        @block.vector
        def _(dve):
            ve = nc.vector
            ve.memset(weff[:, TQ, :, :], 0.0).then_inc(pad_zero, 1)
            ve.memset(eps_sb[:, :], EPS).then_inc(eps_set, 1)
            dve.wait_ge(weff_mm, 1)
            src = bank[2][0:C, :].rearrange("p (o h q u) -> p q u h o", h=2, q=2, u=TQ)
            for q in range(2):
                ve.tensor_copy(weff[q * C:(q + 1) * C, 0:TQ, :, 0:D // 2], src[:, q, :, :, :]).then_inc(weff_done, 1)
            dve.wait_ge(weff_act, 2)
            dve.wait_ge(pad_zero, 1)
            for k in range(2):
                src = bank[2 + k][0:C, :].rearrange("p (o h r) -> p o h r", h=2, r=STRIDE)
                ve.tensor_reduce(weff[C:128, TQ, 1, D // 2 * k:D // 2 * (k + 1)], src[:, :, 1, :], AX_X,
                                 ALU.add).then_inc(pad_sum, 1)
            dve.wait_ge(route_in, 16)
            ve.tensor_copy(route_f[:, :], route_sb[:, :]).then_inc(route_cast, 1)
            dve.wait_ge(route_cast, 1)
            dve.wait_ge(small_in, 16)
            ve.tensor_scalar(onehot[:, :], route_f[:, :], packed("expert_ids", NE), None,
                             ALU.is_equal).then_inc(onehot_done, 1)
            ve.tensor_tensor(wres[:, :, :], packed("wsh").rearrange("p (l h) -> p l h", l=NL),
                             ident.unsqueeze(1).broadcast_to([HID, NL, HID]), ALU.add).then_inc(wres_done, 1)

            def second_part(t):
                b = t // 2
                dve.wait_ge(tok_mm, t + 1)
                src = tok_bank[t][C:128, :].rearrange("p (k v) -> p v k", k=HB)
                if t % 2:
                    ve.tensor_copy(y_sb[C:128, b, :, HB - 1:NPATCH - 1], src).then_inc(y_second, 1)
                else:
                    ve.tensor_copy(y_sb[C:128, b, :, 0:HB - 1], src[:, :, 1:HB]).then_inc(y_second, 1)

            def padding(b):
                dve.wait_ge(pad_mm, b + 1)
                ve.tensor_copy(y_sb[C:128, b, :, NPATCH - 1], pad_ps[C:128, b, :]).then_inc(y_pad, 1)

            def small_copies():
                dve.wait_ge(setup_mm, 1)
                ve.tensor_copy(packed("wvc"), wvc_ps).then_inc(wvc_done, 1)
                ve.tensor_copy(wo_c[:, :], woc_ps).then_inc(setup_done, 1)
                ve.tensor_copy(bo_c[:, :], boc_ps).then_inc(setup_done, 1)
                ve.tensor_tensor(bias[:, :, :], bias_ps, packed("b_sh").unsqueeze(2).broadcast_to([HID, NL, NG]),
                                 ALU.add).then_inc(setup_done, 1)

            def rotate(u):
                i = u % UB * UC
                cos, sin = rope_sb[:, 0, i:i + UC, :], rope_sb[:, 1, i:i + UC, :]
                dve.wait_ge(qk_mm, u + 1)
                if u == 0:
                    dve.wait_ge(rope_in, 16)
                ve.tensor_tensor(qk[:, u, :, :], qk_ps, cos, ALU.mult).then_inc(rope_parts, 1)
                if u >= 2:
                    dve.wait_ge(rope_done, u - 1)
                pairs = qk_ps.rearrange("p c (i two) -> p (c i) two", two=2)[:, :, ::-1]
                ve.tensor_tensor(rope_tmp[:, u % 2, :, :].rearrange("p c (i two) -> p (c i) two", two=2), pairs,
                                 sin.rearrange("p c (i two) -> p (c i) two", two=2), ALU.mult).then_inc(rope_parts, 1)
                dve.wait_ge(rope_parts, 2 * u + 2)
                ve.tensor_tensor(qk[:, u, :, :], qk[:, u, :, :], rope_tmp[:, u % 2, :, :],
                                 ALU.add).then_inc(rope_done, 1)

            def keys(u):
                dve.wait_ge(qkT_mm, u + 1)
                if u >= 2:
                    dve.wait_ge(score_mm, u - 1)
                ve.tensor_copy(kT[:, u % 2, :], qkT_ps[D:2 * D, :]).then_inc(kT_done, 1)

            def mask_scores(u):
                dve.wait_ge(score_mm, u + 1)
                if u >= 2:
                    dve.wait_ge(norm_mm, turn(NORMS, RET, u - 2))
                ve.tensor_tensor(sT[:, u % 2, :, :], sT_ps, mask.unsqueeze(1).broadcast_to([128, UC, CH]),
                                 ALU.mult).then_inc(masked, 1)
                for c in range(UC):
                    s = u // UB * NCH + u % UB * UC + c
                    if not has_state(u, c):
                        continue
                    if s % NCH == 0:
                        ve.tensor_copy(state[:, s, :], state_ps[:, c, :]).then_inc(state_done, 1)
                    else:
                        dve.wait_ge(state_done, states_before(u) + c)
                        ve.scalar_tensor_tensor(state[:, s, :], state[:, s - 1, :], STATE_DECAY, state_ps[:, c, :],
                                                ALU.mult, ALU.add).then_inc(state_done, 1)

            def norm_sum(k, u):
                n = turn(NORMS, k, u)
                dve.wait_ge(norm_mm, n)
                if k == RET:
                    residual = vh[:, u, :, D:2 * D]
                    dve.wait_ge(vh_done, u + 1)
                else:
                    residual = h1b[:, u, :, :]
                    dve.wait_ge(h1b_done, u + 1)
                ve.tensor_tensor(hsum[:, n % 2, :, :], norm_ps, residual, ALU.add).then_inc(sum_done, 1)

            def norm_scale(k, u):
                n = turn(NORMS, k, u)
                dve.wait_ge(sd_done, n)
                ve.reciprocal(stat[:, n - 1, 2, :], stat[:, n - 1, 1, :]).then_inc(rstd_done, 1)
                dve.wait_ge(rstd_done, n)
                ve.tensor_tensor((h1 if k == RET else res)[:, u, :, :], hsum[:, n % 2, :, :],
                                 stat[:, n - 1, 2, :].unsqueeze(2).broadcast_to([128, UC, D]),
                                 ALU.mult).then_inc(norm_done, 1)

            def add_bias(l, k, u):
                dve.wait_ge(layerT_mm, turn(LAYER_T, k, u))
                if u >= 2 and l == 0:
                    dve.wait_ge(layer_mm, turn(LAYER, L1, u - 2))
                if u >= 2 and l == 1:
                    dve.wait_ge(norm_mm, turn(NORMS, OUT, u - 2))
                b_g = bias[:, l, u * UG:(u + 1) * UG].unsqueeze(2).broadcast_to([HID, UG, GT])
                ve.tensor_tensor(hid[:, 1 + l, u % 2, :].rearrange("p (g t) -> p g t", g=UG),
                                 ring(k, u).rearrange("p (g t) -> p g t", g=UG), b_g, ALU.add).then_inc(biased, 1)

            second_part(0)
            second_part(1)
            padding(0)
            small_copies()
            second_part(2)
            for k, u in wave():
                if (k, u) == (SCORE, 0):
                    second_part(3)
                    padding(1)
                if k == PROJ:
                    rotate(u)
                elif k == QKT:
                    keys(u)
                elif k == SCORE:
                    mask_scores(u)
                elif k in NORMS:
                    norm_sum(k, u)
                    norm_scale(k, u)
                elif k in LAYER_T:
                    add_bias(LAYER_T.index(k), k, u)

        @block.scalar
        def _(act):
            se = nc.scalar
            act.wait_ge(weff_mm, 1)
            src = bank[3][0:C, :].rearrange("p (o h q u) -> p q u h o", h=2, q=2, u=TQ)
            for q in range(2):
                se.copy(weff[q * C:(q + 1) * C, 0:TQ, :, D // 2:D], src[:, q, :, :, :]).then_inc(weff_act, 1)

            def first_part(t):
                act.wait_ge(tok_mm, t + 1)
                k0 = t % 2 * HB
                se.copy(y_sb[0:C, t // 2, :, k0:k0 + HB],
                        tok_bank[t][0:C, :].rearrange("p (k v) -> p v k", k=HB)).then_inc(y_first, 1)

            def values(u):
                act.wait_ge(vh_mm, u + 1)
                se.copy(vh[:, u, :, :], vh_ps).then_inc(vh_done, 1)

            def queries(u):
                act.wait_ge(qkT_mm, u + 1)
                if u >= QTS:
                    act.wait_ge(norm_mm, turn(NORMS, RET, u - QTS))
                se.copy(qT[:, u % QTS, :], qkT_ps[0:D, :]).then_inc(qT_done, 1)

            def norm(k, u):
                n = turn(NORMS, k, u)
                act.wait_ge(sum_done, n)
                for c in range(UC):
                    se.activation(sq[:, n % 2, c, :], hsum[:, n % 2, c, :], ACT.Square, scale=1.0 / D ** 0.5,
                                  accum_out=stat[:, n - 1, 0, c:c + 1]).then_inc(var_done, 1)
                act.wait_ge(var_done, UC * n)
                se.activation(stat[:, n - 1, 1, :], stat[:, n - 1, 0, :], ACT.Sqrt, bias=eps_sb[:, 0:1]).then_inc(sd_done, 1)

            def copy_h1T(u):
                act.wait_ge(h1T_mm, u + 1)
                if u >= 2:
                    act.wait_ge(in_mm, u - 1)
                se.copy(h1T[:, u % 2, :], h1T_ps).then_inc(h1T_done, 1)

            def relu_in(u):
                act.wait_ge(in_mm, u + 1)
                if u >= 2:
                    act.wait_ge(layer_mm, turn(LAYER, L0, u - 2))
                se.activation(hid[:, 0, u % 2, :], ring(IN, u), ACT.Relu, bias=packed("b_in")).then_inc(in_done, 1)

            def copy_z(l, k, u):
                act.wait_ge(layer_mm, turn(LAYER, k, u))
                if u >= 2:
                    act.wait_ge(layerT_mm, turn(LAYER_T, LAYER_T[l], u - 2))
                se.copy(z[:, l, u % 2, :, :], ring(k, u).rearrange("p (c h) -> p c h", c=UC)).then_inc(z_done, 1)

            def relu(l, k, u):
                act.wait_ge(biased, turn(LAYER_T, k, u))
                h = hid[:, 1 + l, u % 2, :]
                se.activation(h, h, ACT.Relu).then_inc(relu_done, 1)

            first_part(0)
            first_part(1)
            first_part(2)
            act.wait_ge(small_in, 16)
            act.wait_ge(eps_set, 1)
            for k, u in wave():
                if (k, u) == (SCORE, 0):
                    first_part(3)
                if k == PROJ:
                    values(u)
                elif k == QKT:
                    queries(u)
                elif k in NORMS:
                    norm(k, u)
                elif k == H1T:
                    copy_h1T(u)
                elif k == IN:
                    relu_in(u)
                elif k in LAYER:
                    copy_z(LAYER.index(k), k, u)
                elif k in LAYER_T:
                    relu(LAYER_T.index(k), k, u)


def kernel(x, L0_tok_W, L0_attn_W_Q, L0_attn_W_K, L0_attn_W_V, L0_ffn_route_id, L0_ffn_Wi, L0_ffn_bi,
           L0_ffn_Wr, L0_ffn_br, L0_ffn_Ws, L0_ffn_bs, L0_ffn_Wo, L0_ffn_bo):
    import concourse.bacc as bacc
    from concourse.bass_utils import run_bass_kernel_spmd

    a = lambda t: np.asarray(t)
    tables = constants()
    w_qk = np.concatenate([a(L0_attn_W_Q), a(L0_attn_W_K)], 1)
    parts = {
        "wqk": np.concatenate([w_qk, w_qk], 0),
        "center": tables["center"],
        "mask": tables["mask"],
        "ident": tables["ident"],
        "wsh": a(L0_ffn_Ws)[:, 0].transpose(2, 0, 1).reshape(HID, NL * HID),
        "wvT": np.concatenate([a(L0_attn_W_V).T] * 2, 1),
        "w_in": a(L0_ffn_Wi).T,
        "w_out": a(L0_ffn_Wo),
        "b_out": np.broadcast_to(a(L0_ffn_bo)[:, None], (D, CH)),
        "b_in": a(L0_ffn_bi)[:, None],
        "b_sh": a(L0_ffn_bs)[:, 0].T,
        "b_routed": a(L0_ffn_br).transpose(1, 0, 2).reshape(NE, NL * HID),
        "expert_ids": tables["expert_ids"],
    }
    small = np.zeros((128, packed_at("expert_ids")[1]), np.float32)
    for name, p in parts.items():
        c0, c1 = packed_at(name)
        small[0:p.shape[0], c0:c1] = p
    arrays = {
        "x": a(x),
        "w_tok": np.concatenate([tables["dft"], a(L0_tok_W).reshape(OG, OS, RF, C).transpose(1, 2, 0, 3)
                                 .reshape(OS * RF, OG * C)], 1),
        "small": small,
        "route": a(L0_ffn_route_id),
        "w_routedT": a(L0_ffn_Wr).transpose(1, 3, 0, 2).reshape(NE, HID, NL * HID),
        "rope": tables["rope"],
    }
    arrays = {k: np.ascontiguousarray(v) for k, v in arrays.items()}
    nc = bacc.Bacc("TRN2", target_bir_lowering=False, num_devices=1)
    aps = {k: nc.dram_tensor(k, v.shape, mybir.dt.from_np(v.dtype), kind="ExternalInput").ap()
           for k, v in arrays.items()}
    aps["out"] = nc.dram_tensor("out", (B, SEQ, D), F32, kind="ExternalOutput").ap()
    build(nc, **aps)
    r = run_bass_kernel_spmd(nc, [arrays], core_ids=[0])
    return r.results[0]["out"]
```

```python
from contextlib import ExitStack

import numpy as np
import concourse.bass as bass
from concourse import mybir

ALU = mybir.AluOpType
ACT = mybir.ActivationFunctionType
AX_X = mybir.AxisListType.X
F32 = mybir.dt.float32
I32 = mybir.dt.int32

B, C, T, V = 2, 64, 128, 64
PATCH, STRIDE = 16, 8
NPATCH = T // STRIDE
SEQ = V * NPATCH
RF = 2 * (PATCH // 2 + 1)
D = 64
OS = 4
OG = D // OS
WG = OG // 4
TQ = STRIDE // 2
HB = NPATCH // 2
VT = V // 2
NT = 2 * B
CH = 128
NCH = SEQ // CH
UC = 2
UB = NCH // UC
NU = B * UB
UT = UC * CH
HID = 128
NL, NE = 2, 16
NG = 64
GT = B * SEQ // NG
CG = CH // GT
HALVES = (slice(0, CH // 2), slice(CH // 2, CH))
WARM = 9
POOL_G = (6, 7)
X_FIRST = 1
UG = UC * CG
GAMMA = 0.96875
THETA = 10000.0
EPS = 1e-5
STATE_DECAY = GAMMA ** CH

PROJ, QKT, SCORE, RET, H1T, IN, L0, L0T, L1, L1T, OUT = range(11)
VAR_H1, VAR_OUT, SCALE_H1, SCALE_OUT, RESIDUAL, WEIGHTS = range(11, 17)
TOK_A, TOK_B, PAD, SMALL = range(17, 21)
RING = (TOK_A, IN, L0, L0T, L1, L1T)
TOK = (TOK_A, TOK_B)
LAYER = (L0, L1)
LAYER_T = (L0T, L1T)
NORMS = (RET, OUT)
VAR = (VAR_H1, VAR_OUT)
SCALE = (SCALE_H1, SCALE_OUT)

LAG = {PROJ: 0.0, QKT: 0.839, SCORE: 1.774, RET: 2.215, H1T: 3.59, IN: 4.105, L0: 5.952,
       L0T: 6.618, L1: 7.311, L1T: 8.047, OUT: 8.777, WEIGHTS: 2.182, RESIDUAL: 4.119}
VAR_LAG, SCALE_LAG = 0.257, 0.589
TOK_AT = ((-1.206, -0.623), (-0.604, 0.579), (0.702, 2.738), (1.718, 3.652))
DVE_LATE = {PROJ: 0.0, SCORE: 0.019, RET: -0.035, OUT: -0.035, L0T: 0.048, L1T: 0.048}
ACT_LATE = {PROJ: 0.248, QKT: 0.0, H1T: -0.312, IN: 0.122, L0: 0.039, L1: 0.039}
PAD_AT = (-0.582, 2.78)
SMALL_AT = -0.121

PACKED = [("wqk", 2 * D), ("wvc", D), ("center", D), ("ident", CH), ("wvT", 2 * D), ("mask", CH),
          ("decay", 4), ("w_out", HID), ("b_out", CH), ("b_in", 1), ("b_sh", NL),
          ("expert_ids", 1), ("w_in", UC * HID), ("wsh", NL * HID)]


def packed_at(name):
    at = 0
    for n, w in PACKED:
        if n == name:
            return at, at + w
        at += w


def timeline(late={}):
    lag = dict(LAG)
    for stages, behind in ((VAR, VAR_LAG), (SCALE, SCALE_LAG)):
        for k, norm in zip(stages, NORMS):
            lag[k] = lag[norm] + behind
    runs = [(at + u + late.get(k, 0.0), k, u) for k, at in lag.items() for u in range(NU)]
    runs += [(at, k, t) for t in range(NT) for k, at in zip(TOK, TOK_AT[t])]
    runs += [(at, PAD, b) for b, at in enumerate(PAD_AT)] + [(SMALL_AT, SMALL, 0)]
    return [(k, u) for _, k, u in sorted(runs)]


def turn(stages, k, u):
    runs = [x for x in timeline() if x[0] in stages]
    return runs.index((k, u)) + 1


def ran(stages, k, u):
    runs = timeline()
    return sum(x[0] in stages for x in runs[:runs.index((k, u))])


def constants():
    f = np.arange(PATCH // 2 + 1)[:, None] * np.arange(PATCH)[None, :] * (2 * np.pi / PATCH)
    dft = np.concatenate([np.cos(f), -np.sin(f)]) / np.sqrt(PATCH)
    dft_blocks = np.zeros((OS, RF, OS, PATCH))
    for s in range(OS):
        dft_blocks[s, :, s, :] = dft
    inv_freq = (1.0 / THETA ** (np.arange(0, D, 2, dtype=np.float32) / np.float32(D))).astype(np.float32)
    angle = (np.arange(SEQ, dtype=np.float32)[:, None] * inv_freq[None, :]).astype(np.float64)
    local = np.arange(CH)
    decay = np.stack([GAMMA ** (local + 1.0), GAMMA ** (CH - 1.0 - local)], 1)
    rope = np.stack([np.cos(angle), np.sin(angle)]).reshape(2, NCH, CH, D // 2).transpose(2, 0, 1, 3)
    key, query = np.arange(CH)[:, None], np.arange(CH)[None, :]
    center = np.eye(D) - 1.0 / D
    f32 = lambda a: np.ascontiguousarray(a, np.float32)
    return {
        "dft": f32(dft_blocks.reshape(OS * RF, OS * PATCH)),
        "rope": f32(rope),
        "decay": f32(np.concatenate([decay, -decay], 1)),
        "mask": f32(np.where(query >= key, GAMMA ** -float(CH), 0.0)),
        "ident": f32(np.eye(CH)),
        "center": f32(np.concatenate([center, center])),
        "expert_ids": f32(np.arange(NE)[:, None]),
    }


def build(nc, x, w_tok, small, route, b_routed, w_routedT, rope, out):
    with ExitStack() as ctx:
        def sb(name, shape, dt=F32):
            return ctx.enter_context(nc.sbuf_tensor(name, shape, dt))

        def sem(name):
            return ctx.enter_context(nc.semaphore(name))

        bank = [ctx.enter_context(nc.psum_tensor(f"bank{i}", [128, 512], F32)) for i in range(8)]

        x_sb = sb("x_sb", [128, B, NPATCH, TQ, V])
        wtok_sb = sb("wtok_sb", [OS * RF, OS * PATCH + OG * C])
        small_sb = sb("small_sb", [128, packed_at("wsh")[1]])
        rope_in_sb = sb("rope_in_sb", [128, 2, NCH, D // 2])
        rope_sb = sb("rope_sb", [128, 2, NCH, 2, D // 2, 2])
        route_sb = sb("route_sb", [NE, NG], I32)
        b_routed_sb = sb("b_routed_sb", [NE, NL, HID])
        experts = sb("experts", [HID, NE, NL, HID])

        def packed(name, rows=128):
            a, b = packed_at(name)
            return small_sb[0:rows, a:b]

        mask, ident = packed("mask"), packed("ident")
        w_qk = packed("wqk")
        w_vh = small_sb[:, packed_at("wvc")[0]:packed_at("center")[1]]

        pad_parts = sb("pad_parts", [128, 2, D])
        weff = sb("weff", [128, TQ + 1, 2, D])
        y_sb = sb("y_sb", [128, B, V, NPATCH])
        qk = sb("qk", [128, NU, UC, 2 * D])
        rope_tmp = sb("rope_tmp", [128, 2, UC, 2 * D])
        vh = sb("vh", [128, NU, UC, 2 * D])
        qT = sb("qT", [D, 3, UT])
        kT = sb("kT", [D, 2, UT])
        sT = sb("sT", [128, 2, UC, CH])
        state = sb("state", [D, B * NCH, D])
        hsum = sb("hsum", [128, 2, UC, D])
        sq = sb("sq", [128, 2, UC, D])
        stat = sb("stat", [128, 2 * NU, 3, UC])
        h1 = sb("h1", [128, NU, UC, D])
        h1b = sb("h1b", [128, NU, UC, D])
        h1T = sb("h1T", [128, 2, CH])
        z = sb("z", [128, NL, 2, UC, HID])
        hid = sb("hid", [HID, NL + 1, 2, UT])
        res = sb("res", [128, NU, UC, D])
        eps_sb = sb("eps_sb", [128, 1])
        zeros = sb("zeros", [128, 512], mybir.dt.bfloat16)
        onehot = sb("onehot", [NE, NG])
        route_f = sb("route_f", [NE, NG])
        bias = sb("bias", [HID, NL, NG])
        wres = sb("wres", [HID, NL, HID])
        wgroup = sb("wgroup", [HID, NG, NL, HID])
        wo_c = sb("wo_c", [HID, D])
        bo_c = sb("bo_c", [128, D])

        wtok_in, x_in = sem("wtok_in"), [sem(f"x_in{i}") for i in range(NT)]
        small_in, late_in, rope_in, route_in = sem("small_in"), sem("late_in"), sem("rope_in"), sem("route_in")
        b_routed_in = sem("b_routed_in")
        experts_in = sem("experts_in")
        stored = sem("stored")
        weff_mm, setup_mm, tok_mm, pad_mm = sem("weff_mm"), sem("setup_mm"), sem("tok_mm"), sem("pad_mm")
        qk_mm, vh_mm, qkT_mm, score_mm = sem("qk_mm"), sem("vh_mm"), sem("qkT_mm"), sem("score_mm")
        norm_mm, h1T_mm, in_mm, layer_mm, layerT_mm = (sem("norm_mm"), sem("h1T_mm"), sem("in_mm"), sem("layer_mm"),
                                                       sem("layerT_mm"))
        weff_done, weff_act, pad_zero = sem("weff_done"), sem("weff_act"), sem("pad_zero")
        pad_part, pad_sum = sem("pad_part"), sem("pad_sum")
        route_cast, onehot_done, wres_done = sem("route_cast"), sem("onehot_done"), sem("wres_done")
        wgroup_pool, wgroup_dve, rope_table = sem("wgroup_pool"), sem("wgroup_dve"), sem("rope_table")
        wvc_done, setup_done = sem("wvc_done"), sem("setup_done")
        y_first, y_second, y_pad = sem("y_first"), sem("y_second"), sem("y_pad")
        rope_parts, rope_done, vh_done = sem("rope_parts"), sem("rope_done"), sem("vh_done")
        qT_done, kT_done, masked, state_done = sem("qT_done"), sem("kT_done"), sem("masked"), sem("state_done")
        sum_done, var_done, eps_set, zeros_set = sem("sum_done"), sem("var_done"), sem("eps_set"), sem("zeros_set")
        sd_done, rstd_done, norm_done, h1b_done = sem("sd_done"), sem("rstd_done"), sem("norm_done"), sem("h1b_done")
        h1T_done, in_done, z_done, biased, relu_done = (sem("h1T_done"), sem("in_done"), sem("z_done"), sem("biased"),
                                                        sem("relu_done"))

        weff_bank = [bank[2], bank[3], bank[4], bank[0]]
        pad_ps = bank[7][:, 0:B * V].rearrange("p (b v) -> p b v", b=B)
        qk_ps = bank[2][:, 0:UC * 2 * D].rearrange("p (c d) -> p c d", c=UC)
        vh_ps = bank[3][:, 0:UC * 2 * D].rearrange("p (c d) -> p c d", c=UC)
        qkT_ps = bank[4][:, 0:UT]
        h1T_ps = bank[4][:, UT:UT + CH]
        sT_ps = bank[5][:, 0:UT].rearrange("p (c n) -> p c n", c=UC)
        state_ps = [bank[5][c * D:(c + 1) * D, UT:UT + D] for c in range(UC)]
        norm_ps = bank[7][:, 0:UC * D].rearrange("p (c d) -> p c d", c=UC)
        ring_bank = [bank[0], bank[1], bank[6]]
        wvc_ps, woc_ps, boc_ps = bank[4][:, 0:D], bank[4][:, D:2 * D], bank[4][:, 2 * D:3 * D]
        bias_ps = bank[4][:, 3 * D:3 * D + NL * NG].rearrange("p (l g) -> p l g", l=NL)

        def ring(k, u):
            return ring_bank[turn(RING, k, u) % 3][:, 0:UT]

        def tok_bank(t):
            return ring_bank[turn(RING, TOK_A, t) % 3]

        def states_before(u):
            return (u // UB) * (NCH - 1) + (u % UB) * UC

        def weff_src(part, q):
            ps = weff_bank[part][0:C, 0:WG * OS * PATCH]
            return ps.rearrange("p (o h q u) -> p q u h o", h=2, q=2, u=TQ)[:, q, :, :, :]

        def weff_dst(part, q):
            return weff[q * C:(q + 1) * C, 0:TQ, :, part * WG * OS:(part + 1) * WG * OS]

        def y_chunk(u, c):
            v0 = (u % UB * UC + c) * CH // NPATCH
            return y_sb[:, u // UB, v0:v0 + CH // NPATCH, :].rearrange("p v n -> p (v n)")

        def pool_groups(u):
            return sum(POOL_G[i // UB] for i in range(u + 1))

        def has_state(u, c):
            return u % UB * UC + c < NCH - 1

        block = ctx.enter_context(nc.Block())

        @block.sync
        def _(sp):
            early = packed_at("w_in")[0]
            xv = x.rearrange("b c (k q u) v -> b q c k (u v)", k=NPATCH, q=2)
            sp.dma_start(wtok_sb[:, :], w_tok).then_inc(wtok_in, 16)

            def load_x(b, half):
                for q in range(2):
                    dst = x_sb[q * C:(q + 1) * C, b, half * HB:(half + 1) * HB, :, :].rearrange("p k u v -> p k (u v)")
                    sp.dma_start(dst, xv[b, q, :, half * HB:(half + 1) * HB, :]).then_inc(x_in[2 * b + half], 16)

            load_x(0, 0)
            load_x(0, 1)
            sp.dma_start(rope_in_sb[:, :, :, :], rope).then_inc(rope_in, 16)
            sp.dma_start(small_sb[:, 0:early], small[:, 0:early]).then_inc(small_in, 16)
            sp.dma_start(small_sb[:, early:], small[:, early:]).then_inc(late_in, 16)
            for half in range(X_FIRST):
                load_x(1, half)
            sp.dma_start(experts[:, :, :, :].rearrange("p e l h -> p e (l h)"),
                         w_routedT.rearrange("e p n -> p e n")).then_inc(experts_in, 16)
            for half in range(X_FIRST, 2):
                load_x(1, half)
            ov = out.rearrange("b (s c p) d -> (b s) p c d", c=UC, p=CH)
            for u in range(NU):
                sp.wait_ge(norm_done, turn(NORMS, OUT, u))
                sp.dma_start(ov[u], res[:, u, :, :]).then_inc(stored, 16)
            sp.wait_ge(stored, 16 * NU)

        @block.gpsimd
        def _(pool):
            pool.dma_start(route_sb[:, :], route.partition_broadcast(NE)).then_inc(route_in, 16)
            pool.dma_start(b_routed_sb[:, :, :], b_routed).then_inc(b_routed_in, 16)
            pool.wait_ge(small_in, 16)
            pool.wait_ge(late_in, 16)
            nc.gpsimd.tensor_tensor(wres[:, :, :], packed("wsh").rearrange("p (l h) -> p l h", l=NL),
                                    ident.unsqueeze(1).broadcast_to([HID, NL, HID]), ALU.add).then_inc(wres_done, 1)
            pool.wait_ge(route_in, 16)
            pool.wait_ge(experts_in, 16)
            pool.wait_ge(wres_done, 1)
            ids = [pool.alloc_register(f"pool_expert{g}") for g in range(UG)]
            for b, share in enumerate(POOL_G):
                with pool.Fori(b * UB, (b + 1) * UB) as u:
                    pool.load(ids[0:share], route_sb[0:1, bass.ds(u * UG, share)])
                    for g in range(share):
                        e = pool.snap(ids[g], min_val=0, max_val=NE - 1)
                        dst = wgroup[:, bass.ds(u * UG + g, 1), :, :].rearrange("p g l h -> p (g l h)")
                        nc.gpsimd.tensor_tensor(dst, experts[:, bass.ds(e, 1), :, :].rearrange("p e l h -> p (e l h)"),
                                                wres[:, :, :].rearrange("p l h -> p (l h)"),
                                                ALU.add).then_inc(wgroup_pool, 1)

        @block.tensor
        def _(pe):
            mm = nc.tensor.matmul

            pe.wait_ge(zeros_set, 1)

            for _ in range(WARM):
                mm(bank[5][:, :], zeros[:, 0:128], zeros[:, :], start=True, stop=True)
            pe.wait_ge(wtok_in, 16)
            for g in range(OG):
                w = wtok_sb[:, OS * PATCH + g * C:OS * PATCH + (g + 1) * C]
                part, i = g // WG, g % WG
                last = mm(weff_bank[part][0:C, i * OS * PATCH:(i + 1) * OS * PATCH], w, wtok_sb[:, 0:OS * PATCH],
                          start=True, stop=True)
                if i == WG - 1:
                    last.then_inc(weff_mm, 1)

            def tokenize(t, half):
                b, v0, k0 = t // 2, t % 2 * VT, half * HB
                pe.wait_ge(x_in[2 * b + half], 32)
                if half == 0:
                    ring_free(TOK_A, t)
                for u in range(TQ):
                    last = mm(tok_bank(t)[:, k0 * VT:(k0 + HB) * VT], weff[:, u, :, :].rearrange("p h o -> p (h o)"),
                              x_sb[:, b, k0:k0 + HB, u, v0:v0 + VT], start=(u == 0), stop=(u == TQ - 1))
                if half:
                    last.then_inc(tok_mm, 1)

            def pad(b):
                if b:
                    pe.wait_ge(y_pad, b)
                else:
                    pe.wait_ge(pad_sum, 1)
                if ran(NORMS, PAD, b):
                    pe.wait_ge(sum_done, ran(NORMS, PAD, b))
                mm(pad_ps[:, b, :], weff[:, TQ, :, :].rearrange("p h o -> p (h o)"),
                   x_sb[:, b, NPATCH - 1, TQ - 1, :], start=True, stop=True).then_inc(pad_mm, 1)

            def small_products():
                pe.wait_ge(small_in, 16)
                pe.wait_ge(onehot_done, 1)
                pe.wait_ge(b_routed_in, 16)
                c1 = packed("center", D)
                mm(wvc_ps, packed("wvT", D), c1, start=True, stop=True)
                mm(woc_ps, packed("w_out", D), c1, start=True, stop=True)
                mm(boc_ps, packed("b_out", D), c1, start=True, stop=True)
                for l in range(NL):
                    last = mm(bias_ps[:, l, :], b_routed_sb[:, l, :], onehot[:, :], start=True, stop=True)
                last.then_inc(setup_mm, 1)

            def project(u):
                tile = u * UC * CH // (VT * NPATCH)
                pe.wait_ge(y_first, tile + 1)
                pe.wait_ge(y_second, tile + 1)
                pe.wait_ge(y_pad, u // UB + 1)
                if u:
                    pe.wait_ge(rope_parts, 2 * u)
                for c in range(UC):
                    last = mm(qk_ps[:, c, :], y_chunk(u, c), w_qk, start=True, stop=True)
                last.then_inc(qk_mm, 1)
                if u:
                    pe.wait_ge(vh_done, u)
                else:
                    pe.wait_ge(wvc_done, 1)
                for c in range(UC):
                    last = mm(vh_ps[:, c, :], y_chunk(u, c), w_vh, start=True, stop=True)
                last.then_inc(vh_mm, 1)

            def transpose_qk(u):
                pe.wait_ge(rope_done, u + 1)
                if u:
                    pe.wait_ge(qT_done, u)
                    pe.wait_ge(kT_done, u)
                else:
                    pe.wait_ge(setup_done, 3)
                if ran((H1T,), QKT, u):
                    pe.wait_ge(h1T_done, ran((H1T,), QKT, u))
                for c in range(UC):
                    last = nc.tensor.transpose(qkT_ps[:, c * CH:(c + 1) * CH], qk[:, u, c, :], ident)
                last.then_inc(qkT_mm, 1)

            def scores(u):
                pe.wait_ge(vh_done, u + 1)
                pe.wait_ge(qT_done, u + 1)
                pe.wait_ge(kT_done, u + 1)
                if u:
                    pe.wait_ge(masked, u)
                    pe.wait_ge(state_done, states_before(u))
                for c in range(UC):
                    if has_state(u, c):
                        mm(state_ps[c], qk[:, u, c, D:2 * D], vh[:, u, c, 0:D], start=True, stop=True)
                for c in range(UC):
                    last = mm(sT_ps[:, c, :], kT[:, u % 2, c * CH:(c + 1) * CH], qT[:, u % 3, c * CH:(c + 1) * CH],
                              start=True, stop=True)
                last.then_inc(score_mm, 1)

            def retention(u):
                pe.wait_ge(masked, u + 1)
                if u:
                    pe.wait_ge(sum_done, turn(NORMS, RET, u) - 1)
                pe.wait_ge(y_pad, ran((PAD,), RET, u))
                for c in range(UC):
                    i = u % UB * UC + c
                    if i:
                        pe.wait_ge(state_done, states_before(u) + c)
                        for rows in HALVES:
                            mm(norm_ps[rows, c, :], qT[:, u % 3, c * CH + rows.start:c * CH + rows.stop],
                               state[:, u // UB * NCH + i - 1, :], start=True, stop=False)
                    for rows in HALVES:
                        last = mm(norm_ps[rows, c, :], sT[:, u % 2, c, rows], vh[:, u, c, 0:D],
                                  start=(i == 0), stop=True)
                last.then_inc(norm_mm, 1)

            def transpose_h1(u):
                pe.wait_ge(norm_done, turn(NORMS, RET, u))
                pe.wait_ge(qT_done, ran((QKT,), H1T, u))
                pe.wait_ge(kT_done, ran((QKT,), H1T, u))
                if u:
                    pe.wait_ge(h1T_done, u)
                nc.tensor.transpose(h1T_ps, h1[:, u, :, :].rearrange("p c d -> p (c d)"), ident).then_inc(h1T_mm, 1)

            def ring_free(k, u):
                n = turn(RING, k, u)
                if n > 3:
                    k0, u0 = [run for run in timeline() if run[0] in RING][n - 4]
                    if k0 == TOK_A:
                        pe.wait_ge(y_first, u0 + 1)
                        pe.wait_ge(y_second, u0 + 1)
                    elif k0 == IN:
                        pe.wait_ge(in_done, u0 + 1)
                    elif k0 in LAYER:
                        pe.wait_ge(z_done, turn(LAYER, k0, u0))
                    else:
                        pe.wait_ge(biased, turn(LAYER_T, k0, u0))

            def ffn_in(u):
                pe.wait_ge(h1T_done, u + 1)
                if u == 0:
                    pe.wait_ge(late_in, 16)
                ring_free(IN, u)
                for c in range(UC):
                    last = mm(ring(IN, u)[:, c * CH:(c + 1) * CH], packed("w_in")[:, c * HID:(c + 1) * HID],
                              h1T[:, u % 2, :], start=True, stop=True)
                last.then_inc(in_mm, 1)

            def layer(l, k, u):
                if l == 0:
                    pe.wait_ge(in_done, u + 1)
                    pe.wait_ge(wgroup_pool, pool_groups(u))
                    pe.wait_ge(wgroup_dve, UG * (u + 1) - pool_groups(u))
                else:
                    pe.wait_ge(relu_done, turn(LAYER_T, L0T, u))
                ring_free(k, u)
                for c in range(UC):
                    ps, h = ring(k, u)[:, c * HID:(c + 1) * HID], hid[:, l, u % 2, c * CH:(c + 1) * CH]
                    for j in range(CG):
                        rows = slice(j * GT, (j + 1) * GT)
                        last = mm(ps[rows, :], h[:, rows], wgroup[:, u * UG + c * CG + j, l, :],
                                  start=True, stop=True)
                last.then_inc(layer_mm, 1)

            def layer_transpose(l, k, u):
                pe.wait_ge(z_done, turn(LAYER, LAYER[l], u))
                ring_free(k, u)
                for c in range(UC):
                    last = nc.tensor.transpose(ring(k, u)[:, c * CH:(c + 1) * CH], z[:, l, u % 2, c, :], ident)
                last.then_inc(layerT_mm, 1)

            def ffn_out(u):
                pe.wait_ge(relu_done, turn(LAYER_T, L1T, u))
                pe.wait_ge(sum_done, turn(NORMS, OUT, u) - 1)
                for c in range(UC):
                    for rows in HALVES:
                        last = mm(norm_ps[rows, c, :], hid[:, NL, u % 2, c * CH + rows.start:c * CH + rows.stop],
                                  wo_c[:, :], start=True, stop=True)
                last.then_inc(norm_mm, 1)

            pe.wait_ge(weff_done, 4)
            pe.wait_ge(weff_act, 4)
            for k, u in timeline():
                if k in TOK:
                    tokenize(u, TOK.index(k))
                elif k == PAD:
                    pad(u)
                elif k == SMALL:
                    small_products()
                elif k == PROJ:
                    project(u)
                elif k == QKT:
                    transpose_qk(u)
                elif k == SCORE:
                    scores(u)
                elif k == RET:
                    retention(u)
                elif k == H1T:
                    transpose_h1(u)
                elif k == IN:
                    ffn_in(u)
                elif k in LAYER:
                    layer(LAYER.index(k), k, u)
                elif k in LAYER_T:
                    layer_transpose(LAYER_T.index(k), k, u)
                elif k == OUT:
                    ffn_out(u)

        @block.vector
        def _(dve):
            ve = nc.vector
            ve.memset(zeros[:, :], 0.0).then_inc(zeros_set, 1)
            ve.memset(weff[:, TQ, :, :], 0.0).then_inc(pad_zero, 1)
            ve.memset(eps_sb[:, :], EPS).then_inc(eps_set, 1)
            for part in (1, 3):
                for q in range(2):
                    dve.wait_ge(weff_mm, part + 1)
                    ve.tensor_copy(weff_dst(part, q), weff_src(part, q)).then_inc(weff_done, 1)
            dve.wait_ge(weff_done, 4)
            dve.wait_ge(weff_act, 4)
            for q in range(2):
                ve.tensor_reduce(pad_parts[C:128, q, :],
                                 weff[q * C:(q + 1) * C, 0:TQ, 1, :].rearrange("p u o -> p o u"), AX_X,
                                 ALU.add).then_inc(pad_part, 1)
            dve.wait_ge(pad_part, 2)
            dve.wait_ge(pad_zero, 1)
            ve.tensor_tensor(weff[C:128, TQ, 1, :], pad_parts[C:128, 0, :], pad_parts[C:128, 1, :],
                             ALU.add).then_inc(pad_sum, 1)
            dve.wait_ge(route_in, 16)
            ve.tensor_copy(route_f[:, :], route_sb[:, :]).then_inc(route_cast, 1)
            dve.wait_ge(route_cast, 1)
            dve.wait_ge(small_in, 16)
            ve.tensor_scalar(onehot[:, :], route_f[:, :], packed("expert_ids", NE), None,
                             ALU.is_equal).then_inc(onehot_done, 1)

            def second_part(t):
                b, v0 = t // 2, t % 2 * VT
                dve.wait_ge(tok_mm, t + 1)
                src = tok_bank(t)[C:128, :].rearrange("p (k v) -> p v k", k=NPATCH)
                ve.tensor_copy(y_sb[C:128, b, v0:v0 + VT, 0:NPATCH - 1], src[:, :, 1:NPATCH]).then_inc(y_second, 1)

            def padding(b):
                dve.wait_ge(pad_mm, b + 1)
                ve.tensor_copy(y_sb[C:128, b, :, NPATCH - 1], pad_ps[C:128, b, :]).then_inc(y_pad, 1)

            def small_copies():
                dve.wait_ge(setup_mm, 1)
                ve.tensor_copy(packed("wvc"), wvc_ps).then_inc(wvc_done, 1)
                ve.tensor_copy(wo_c[:, :], woc_ps).then_inc(setup_done, 1)
                ve.tensor_copy(bo_c[:, :], boc_ps).then_inc(setup_done, 1)
                ve.tensor_tensor(bias[:, :, :], bias_ps, packed("b_sh").unsqueeze(2).broadcast_to([HID, NL, NG]),
                                 ALU.add).then_inc(setup_done, 1)

            def rotate(u):
                i = u % UB * UC
                cos, sin = (rope_sb[:, part, i:i + UC, :, :, :].rearrange("p c j i two -> p c (j i two)")
                            for part in range(2))
                dve.wait_ge(qk_mm, u + 1)
                if u == 0:
                    dve.wait_ge(rope_table, 8)
                ve.tensor_tensor(qk[:, u, :, :], qk_ps, cos, ALU.mult).then_inc(rope_parts, 1)
                if u >= 2:
                    dve.wait_ge(rope_done, u - 1)
                pairs = qk_ps.rearrange("p c (i two) -> p (c i) two", two=2)[:, :, ::-1]
                ve.tensor_tensor(rope_tmp[:, u % 2, :, :].rearrange("p c (i two) -> p (c i) two", two=2), pairs,
                                 sin.rearrange("p c (i two) -> p (c i) two", two=2), ALU.mult).then_inc(rope_parts, 1)
                dve.wait_ge(rope_parts, 2 * u + 2)
                ve.tensor_tensor(qk[:, u, :, :], qk[:, u, :, :], rope_tmp[:, u % 2, :, :],
                                 ALU.add).then_inc(rope_done, 1)

            def mask_scores(u):
                dve.wait_ge(score_mm, u + 1)
                if u >= 2:
                    dve.wait_ge(norm_mm, turn(NORMS, RET, u - 2))
                ve.tensor_tensor(sT[:, u % 2, :, :], sT_ps, mask.unsqueeze(1).broadcast_to([128, UC, CH]),
                                 ALU.mult).then_inc(masked, 1)
                for c in range(UC):
                    s = u // UB * NCH + u % UB * UC + c
                    if not has_state(u, c):
                        continue
                    if s % NCH == 0:
                        ve.tensor_copy(state[:, s, :], state_ps[c]).then_inc(state_done, 1)
                    else:
                        dve.wait_ge(state_done, states_before(u) + c)
                        ve.scalar_tensor_tensor(state[:, s, :], state[:, s - 1, :], STATE_DECAY, state_ps[c],
                                                ALU.mult, ALU.add).then_inc(state_done, 1)

            def norm_sum(k, u):
                n = turn(NORMS, k, u)
                dve.wait_ge(norm_mm, n)
                if k == RET:
                    residual = vh[:, u, :, D:2 * D]
                    dve.wait_ge(vh_done, u + 1)
                else:
                    residual = h1b[:, u, :, :]
                    dve.wait_ge(h1b_done, u + 1)
                ve.tensor_tensor(hsum[:, n % 2, :, :], norm_ps, residual, ALU.add).then_inc(sum_done, 1)

            def norm_scale(k, u):
                n = turn(NORMS, k, u)
                dve.wait_ge(sd_done, n)
                ve.reciprocal(stat[:, n - 1, 2, :], stat[:, n - 1, 1, :]).then_inc(rstd_done, 1)
                dve.wait_ge(rstd_done, n)
                ve.tensor_tensor((h1 if k == RET else res)[:, u, :, :], hsum[:, n % 2, :, :],
                                 stat[:, n - 1, 2, :].unsqueeze(2).broadcast_to([128, UC, D]),
                                 ALU.mult).then_inc(norm_done, 1)

            def add_bias(l, k, u):
                dve.wait_ge(layerT_mm, turn(LAYER_T, k, u))
                if u >= 2 and l == 0:
                    dve.wait_ge(layer_mm, turn(LAYER, L1, u - 2))
                if u >= 2 and l == 1:
                    dve.wait_ge(norm_mm, turn(NORMS, OUT, u - 2))
                b_g = bias[:, l, u * UG:(u + 1) * UG].unsqueeze(2).broadcast_to([HID, UG, GT])
                ve.tensor_tensor(hid[:, 1 + l, u % 2, :].rearrange("p (g t) -> p g t", g=UG),
                                 ring(k, u).rearrange("p (g t) -> p g t", g=UG), b_g, ALU.add).then_inc(biased, 1)
                dve.wait_ge(biased, turn(LAYER_T, k, u))
                h = hid[:, 1 + l, u % 2, :]
                ve.tensor_scalar(h, h, 0.0, None, ALU.max).then_inc(relu_done, 1)

            def residual2(u):
                dve.wait_ge(norm_done, turn(NORMS, RET, u))
                ve.tensor_tensor(h1b[:, u, :, :], h1[:, u, :, :], bo_c[:, :].unsqueeze(1).broadcast_to([128, UC, D]),
                                 ALU.add).then_inc(h1b_done, 1)

            def group_weights(u):
                if u == 0:
                    dve.wait_ge(wres_done, 1)
                    dve.wait_ge(experts_in, 16)
                share = POOL_G[u // UB]
                dve.load(ids[0:UG - share], route_sb[0:1, u * UG + share:(u + 1) * UG])
                for g in range(share, UG):
                    e = dve.snap(ids[g - share], min_val=0, max_val=NE - 1)
                    ve.tensor_tensor(wgroup[:, u * UG + g, :, :].rearrange("p l h -> p (l h)"),
                                     experts[:, bass.ds(e, 1), :, :].rearrange("p e l h -> p (e l h)"),
                                     wres[:, :, :].rearrange("p l h -> p (l h)"), ALU.add).then_inc(wgroup_dve, 1)

            ids = [dve.alloc_register(f"dve_expert{g}") for g in range(UG)]
            for k, u in timeline(DVE_LATE):
                if k == TOK_B:
                    second_part(u)
                elif k == PAD:
                    padding(u)
                elif k == SMALL:
                    small_copies()
                elif k == PROJ:
                    rotate(u)
                elif k == SCORE:
                    mask_scores(u)
                elif k in NORMS:
                    norm_sum(k, u)
                elif k in SCALE:
                    norm_scale(NORMS[SCALE.index(k)], u)
                elif k == RESIDUAL:
                    residual2(u)
                elif k == WEIGHTS:
                    group_weights(u)
                elif k in LAYER_T:
                    add_bias(LAYER_T.index(k), k, u)

        @block.scalar
        def _(act):
            se = nc.scalar
            for part in (0, 2):
                for q in range(2):
                    act.wait_ge(weff_mm, part + 1)
                    se.copy(weff_dst(part, q), weff_src(part, q)).then_inc(weff_act, 1)

            def rope_tables():
                act.wait_ge(rope_in, 16)
                act.wait_ge(small_in, 16)
                decay = packed("decay")
                for part in range(2):
                    for j in range(2):
                        for i in range(2):
                            col = j + (2 if part == 1 and i == 0 else 0)
                            se.mul(rope_sb[:, part, :, j, :, i], rope_in_sb[:, part, :, :],
                                   decay[:, col:col + 1]).then_inc(rope_table, 1)

            def first_part(t):
                act.wait_ge(tok_mm, t + 1)
                v0 = t % 2 * VT
                se.copy(y_sb[0:C, t // 2, v0:v0 + VT, :],
                        tok_bank(t)[0:C, :].rearrange("p (k v) -> p v k", k=NPATCH)).then_inc(y_first, 1)

            def values(u):
                act.wait_ge(vh_mm, u + 1)
                se.copy(vh[:, u, :, :], vh_ps).then_inc(vh_done, 1)

            def queries(u):
                act.wait_ge(qkT_mm, u + 1)
                if u >= 3:
                    act.wait_ge(norm_mm, turn(NORMS, RET, u - 3))
                se.copy(qT[:, u % 3, :], qkT_ps[0:D, :]).then_inc(qT_done, 1)
                if u >= 2:
                    act.wait_ge(score_mm, u - 1)
                se.copy(kT[:, u % 2, :], qkT_ps[D:2 * D, :]).then_inc(kT_done, 1)

            def norm(k, u):
                n = turn(NORMS, k, u)
                act.wait_ge(sum_done, n)
                for c in range(UC):
                    se.activation(sq[:, n % 2, c, :], hsum[:, n % 2, c, :], ACT.Square, scale=1.0 / D ** 0.5,
                                  accum_out=stat[:, n - 1, 0, c:c + 1]).then_inc(var_done, 1)
                act.wait_ge(var_done, UC * n)
                se.activation(stat[:, n - 1, 1, :], stat[:, n - 1, 0, :], ACT.Sqrt, bias=eps_sb[:, 0:1]).then_inc(sd_done, 1)

            def copy_h1T(u):
                act.wait_ge(h1T_mm, u + 1)
                if u >= 2:
                    act.wait_ge(in_mm, u - 1)
                se.copy(h1T[:, u % 2, :], h1T_ps).then_inc(h1T_done, 1)

            def relu_in(u):
                act.wait_ge(in_mm, u + 1)
                if u == 0:
                    act.wait_ge(small_in, 16)
                if u >= 2:
                    act.wait_ge(layer_mm, turn(LAYER, L0, u - 2))
                se.activation(hid[:, 0, u % 2, :], ring(IN, u), ACT.Relu, bias=packed("b_in")).then_inc(in_done, 1)

            def copy_z(l, k, u):
                act.wait_ge(layer_mm, turn(LAYER, k, u))
                if u >= 2:
                    act.wait_ge(layerT_mm, turn(LAYER_T, LAYER_T[l], u - 2))
                se.copy(z[:, l, u % 2, :, :], ring(k, u).rearrange("p (c h) -> p c h", c=UC)).then_inc(z_done, 1)

            act.wait_ge(eps_set, 1)
            for k, u in timeline(ACT_LATE):
                if k == TOK_B:
                    first_part(u)
                elif k == SMALL:
                    rope_tables()
                elif k == PROJ:
                    values(u)
                elif k == QKT:
                    queries(u)
                elif k in VAR:
                    norm(NORMS[VAR.index(k)], u)
                elif k == H1T:
                    copy_h1T(u)
                elif k == IN:
                    relu_in(u)
                elif k in LAYER:
                    copy_z(LAYER.index(k), k, u)


def kernel(x, L0_tok_W, L0_attn_W_Q, L0_attn_W_K, L0_attn_W_V, L0_ffn_route_id, L0_ffn_Wi, L0_ffn_bi,
           L0_ffn_Wr, L0_ffn_br, L0_ffn_Ws, L0_ffn_bs, L0_ffn_Wo, L0_ffn_bo):
    import concourse.bacc as bacc
    from concourse.bass_utils import run_bass_kernel_spmd

    a = lambda t: np.asarray(t)
    tables = constants()
    w_qk = np.concatenate([a(L0_attn_W_Q), a(L0_attn_W_K)], 1)
    w_in = a(L0_ffn_Wi).T
    zero = np.zeros_like(w_in)
    parts = {
        "wqk": np.concatenate([w_qk, w_qk], 0),
        "center": tables["center"],
        "mask": tables["mask"],
        "decay": tables["decay"],
        "ident": tables["ident"],
        "wsh": a(L0_ffn_Ws)[:, 0].transpose(2, 0, 1).reshape(HID, NL * HID),
        "wvT": np.concatenate([a(L0_attn_W_V).T] * 2, 1),
        "w_in": np.block([[w_in, zero], [zero, w_in]]),
        "w_out": a(L0_ffn_Wo),
        "b_out": np.broadcast_to(a(L0_ffn_bo)[:, None], (D, CH)),
        "b_in": a(L0_ffn_bi)[:, None],
        "b_sh": a(L0_ffn_bs)[:, 0].T,
        "expert_ids": tables["expert_ids"],
    }
    small = np.zeros((128, packed_at("wsh")[1]), np.float32)
    for name, p in parts.items():
        c0, c1 = packed_at(name)
        small[0:p.shape[0], c0:c1] = p
    arrays = {
        "x": a(x),
        "w_tok": np.concatenate([tables["dft"], a(L0_tok_W).reshape(OG, OS, RF, C).transpose(1, 2, 0, 3)
                                 .reshape(OS * RF, OG * C)], 1),
        "small": small,
        "route": a(L0_ffn_route_id),
        "b_routed": a(L0_ffn_br).transpose(1, 0, 2),
        "w_routedT": a(L0_ffn_Wr).transpose(1, 3, 0, 2).reshape(NE, HID, NL * HID),
        "rope": tables["rope"],
    }
    arrays = {k: np.ascontiguousarray(v) for k, v in arrays.items()}
    nc = bacc.Bacc("TRN2", target_bir_lowering=False, num_devices=1)
    aps = {k: nc.dram_tensor(k, v.shape, mybir.dt.from_np(v.dtype), kind="ExternalInput").ap()
           for k, v in arrays.items()}
    aps["out"] = nc.dram_tensor("out", (B, SEQ, D), F32, kind="ExternalOutput").ap()
    build(nc, **aps)
    r = run_bass_kernel_spmd(nc, [arrays], core_ids=[0])
    return r.results[0]["out"]
```
